# Optimizing a Trainium2 kernel written in Bass

```python
import numpy as np
import jax
import jax.numpy as jnp

def _softmax(x, axis=-1):
    return jax.nn.softmax(x, axis=axis)

def _gelu(x):
    return jax.nn.gelu(x, approximate=True)

def _silu(x):
    return jax.nn.silu(x)

def _sigmoid(x):
    return jax.nn.sigmoid(x)

def _layernorm(x, axis=-1, eps=1e-05):
    m = jnp.mean(x, axis=axis, keepdims=True)
    v = jnp.var(x, axis=axis, keepdims=True)
    return (x - m) / jnp.sqrt(v + eps)

def _scatter_add(tgt, idx, src, axis=0):
    return tgt.at[idx].add(src)

def _segment_sum(src, seg, n):
    return jax.ops.segment_sum(src, seg, n)
kernel_name = 'mk_sandwich_d1_jaxref_r4_9d045a'

def setup_inputs(seed: int=0):
    np.random.seed(seed)
    _w = jnp.asarray

    def _L0_attn_setup():
        import jax, jax.numpy as jnp
        import numpy as np
        D_MODEL = 256
        ED = 512
        N = 16
        DT_RANK = 64
        K = 4
        B_SZ = 4
        L = 128

        def _causal_depthwise_conv(u, w, b):
            xc = jnp.transpose(u, (0, 2, 1))
            xc = jax.lax.conv_general_dilated(xc, w, window_strides=(1,), padding=[(K - 1, 0)], feature_group_count=ED, dimension_numbers=('NCH', 'OIH', 'NCH'))
            xc = xc + b[None, :, None]
            return jnp.transpose(xc, (0, 2, 1))

        def _ssm_branch(xz_half, z, conv_w, conv_b, Wx, Wdt, b_dt, A_log, Dp):
            x = jax.nn.silu(_causal_depthwise_conv(xz_half, conv_w, conv_b))
            dbc = x @ Wx.T
            delta = dbc[..., :DT_RANK]
            Bm = dbc[..., DT_RANK:DT_RANK + N]
            Cm = dbc[..., DT_RANK + N:]
            delta = jax.nn.softplus(delta @ Wdt.T + b_dt)
            A = -jnp.exp(A_log)
            dA = jnp.exp(delta[..., None] * A)
            bx = delta[..., None] * Bm[:, :, None, :] * x[..., None]
            dA_t = jnp.transpose(dA, (1, 0, 2, 3))
            bx_t = jnp.transpose(bx, (1, 0, 2, 3))
            c_t = jnp.transpose(Cm, (1, 0, 2))
            h0 = jnp.zeros((x.shape[0], ED, N), dtype=x.dtype)

            def step(h, inp):
                dAi, bxi, ci = inp
                h = dAi * h + bxi
                return (h, jnp.einsum('ben,bn->be', h, ci))
            _, ys = jax.lax.scan(step, h0, (dA_t, bx_t, c_t))
            y = jnp.transpose(ys, (1, 0, 2)) + Dp * x
            return y * jax.nn.silu(z)

        def _mamba_block(x, W_in, conv_w, conv_b, Wx, Wdt, b_dt, A_log, Dp, conv_w_b, conv_b_b, Wx_b, Wdt_b, b_dt_b, A_log_b, Dp_b, W_out):
            xz = x @ W_in.T
            xf, zf = (xz[..., :ED], xz[..., ED:])
            y = _ssm_branch(xf, zf, conv_w, conv_b, Wx, Wdt, b_dt, A_log, Dp)
            xz_r = xz[:, ::-1, :]
            xb, zb = (xz_r[..., :ED], xz_r[..., ED:])
            y_b = _ssm_branch(xb, zb, conv_w_b, conv_b_b, Wx_b, Wdt_b, b_dt_b, A_log_b, Dp_b)
            y = (y + y_b[:, ::-1, :]) * 0.5
            return y @ W_out.T
        key = jax.random.key(seed)
        ks = jax.random.split(key, 20)
        s = lambda k, shp, sc: jax.random.normal(k, shp, dtype=jnp.float32) * sc
        dt = jnp.exp(jax.random.uniform(ks[15], (ED,)) * (np.log(0.1) - np.log(0.001)) + np.log(0.001))
        dt = jnp.clip(dt, 0.0001, None)
        inv_dt = dt + jnp.log(-jnp.expm1(-dt))
        A_init = jnp.log(jnp.tile(jnp.arange(1, N + 1, dtype=jnp.float32), (ED, 1)))
        return {'x': s(ks[0], (B_SZ, L, D_MODEL), 1.0), 'W_in': s(ks[1], (2 * ED, D_MODEL), D_MODEL ** (-0.5)), 'conv_w': s(ks[2], (ED, 1, K), K ** (-0.5)), 'conv_b': s(ks[3], (ED,), 0.02), 'Wx': s(ks[4], (DT_RANK + 2 * N, ED), ED ** (-0.5)), 'Wdt': jax.random.uniform(ks[5], (ED, DT_RANK), minval=-DT_RANK ** (-0.5), maxval=DT_RANK ** (-0.5)), 'b_dt': inv_dt, 'A_log': A_init, 'Dp': jnp.ones((ED,), dtype=jnp.float32), 'conv_w_b': s(ks[6], (ED, 1, K), K ** (-0.5)), 'conv_b_b': s(ks[7], (ED,), 0.02), 'Wx_b': s(ks[8], (DT_RANK + 2 * N, ED), ED ** (-0.5)), 'Wdt_b': jax.random.uniform(ks[9], (ED, DT_RANK), minval=-DT_RANK ** (-0.5), maxval=DT_RANK ** (-0.5)), 'b_dt_b': inv_dt, 'A_log_b': A_init, 'Dp_b': jnp.ones((ED,), dtype=jnp.float32), 'W_out': s(ks[10], (D_MODEL, ED), ED ** (-0.5))}
    _L0_attn_in = _L0_attn_setup()

    def _L0_ffn_setup():
        import jax, jax.numpy as jnp
        import numpy as np
        D = 256
        H = 512
        E = 8
        TOP_K = 2
        N_SHARED = 1
        B, S = (2, 256)
        key = jax.random.key(seed)
        ks = jax.random.split(key, 12)
        sc = 0.02
        return {'hidden': jax.random.normal(ks[0], (B, S, D), jnp.float32), 'router_w': jax.random.normal(ks[1], (D, E), jnp.float32) * sc, 'router_b': jnp.zeros((E,), jnp.float32), 'sw1': jax.random.normal(ks[2], (D, H), jnp.float32) * sc, 'sb1': jnp.zeros((H,), jnp.float32), 'sw2': jax.random.normal(ks[3], (H, D), jnp.float32) * sc, 'sb2': jnp.zeros((D,), jnp.float32), 'rw1': jax.random.normal(ks[4], (E, D, H), jnp.float32) * sc, 'rb1': jnp.zeros((E, H), jnp.float32), 'rw2': jax.random.normal(ks[5], (E, H, D), jnp.float32) * sc, 'rb2': jnp.zeros((E, D), jnp.float32)}
    _L0_ffn_in = _L0_ffn_setup()
    _d = {'L0_attn_x': _L0_attn_in['x'], 'L0_attn_W_in': _L0_attn_in['W_in'], 'L0_attn_conv_w': _L0_attn_in['conv_w'], 'L0_attn_conv_b': _L0_attn_in['conv_b'], 'L0_attn_Wx': _L0_attn_in['Wx'], 'L0_attn_Wdt': _L0_attn_in['Wdt'], 'L0_attn_b_dt': _L0_attn_in['b_dt'], 'L0_attn_A_log': _L0_attn_in['A_log'], 'L0_attn_Dp': _L0_attn_in['Dp'], 'L0_attn_conv_w_b': _L0_attn_in['conv_w_b'], 'L0_attn_conv_b_b': _L0_attn_in['conv_b_b'], 'L0_attn_Wx_b': _L0_attn_in['Wx_b'], 'L0_attn_Wdt_b': _L0_attn_in['Wdt_b'], 'L0_attn_b_dt_b': _L0_attn_in['b_dt_b'], 'L0_attn_A_log_b': _L0_attn_in['A_log_b'], 'L0_attn_Dp_b': _L0_attn_in['Dp_b'], 'L0_attn_W_out': _L0_attn_in['W_out'], 'L0_ffn_router_w': _L0_ffn_in['router_w'], 'L0_ffn_router_b': _L0_ffn_in['router_b'], 'L0_ffn_sw1': _L0_ffn_in['sw1'], 'L0_ffn_sb1': _L0_ffn_in['sb1'], 'L0_ffn_sw2': _L0_ffn_in['sw2'], 'L0_ffn_sb2': _L0_ffn_in['sb2'], 'L0_ffn_rw1': _L0_ffn_in['rw1'], 'L0_ffn_rb1': _L0_ffn_in['rb1'], 'L0_ffn_rw2': _L0_ffn_in['rw2'], 'L0_ffn_rb2': _L0_ffn_in['rb2']}
    _x0 = _d['L0_attn_x']
    _d['L0_attn_x'] = jax.random.normal(jax.random.fold_in(jax.random.key(seed), 1), (8, 1024, 256), dtype=_x0.dtype)
    del _x0
    return _d

def reference(L0_attn_x, L0_attn_W_in, L0_attn_conv_w, L0_attn_conv_b, L0_attn_Wx, L0_attn_Wdt, L0_attn_b_dt, L0_attn_A_log, L0_attn_Dp, L0_attn_conv_w_b, L0_attn_conv_b_b, L0_attn_Wx_b, L0_attn_Wdt_b, L0_attn_b_dt_b, L0_attn_A_log_b, L0_attn_Dp_b, L0_attn_W_out, L0_ffn_router_w, L0_ffn_router_b, L0_ffn_sw1, L0_ffn_sb1, L0_ffn_sw2, L0_ffn_sb2, L0_ffn_rw1, L0_ffn_rb1, L0_ffn_rw2, L0_ffn_rb2):

    def _L0_attn_ref(x, W_in, conv_w, conv_b, Wx, Wdt, b_dt, A_log, Dp, conv_w_b, conv_b_b, Wx_b, Wdt_b, b_dt_b, A_log_b, Dp_b, W_out):
        import jax, jax.numpy as jnp
        import numpy as np
        D_MODEL = 256
        ED = 512
        N = 16
        DT_RANK = 64
        K = 4
        B_SZ = 4
        L = 128

        def _causal_depthwise_conv(u, w, b):
            xc = jnp.transpose(u, (0, 2, 1))
            xc = jax.lax.conv_general_dilated(xc, w, window_strides=(1,), padding=[(K - 1, 0)], feature_group_count=ED, dimension_numbers=('NCH', 'OIH', 'NCH'))
            xc = xc + b[None, :, None]
            return jnp.transpose(xc, (0, 2, 1))

        def _ssm_branch(xz_half, z, conv_w, conv_b, Wx, Wdt, b_dt, A_log, Dp):
            x = jax.nn.silu(_causal_depthwise_conv(xz_half, conv_w, conv_b))
            dbc = x @ Wx.T
            delta = dbc[..., :DT_RANK]
            Bm = dbc[..., DT_RANK:DT_RANK + N]
            Cm = dbc[..., DT_RANK + N:]
            delta = jax.nn.softplus(delta @ Wdt.T + b_dt)
            A = -jnp.exp(A_log)
            dA = jnp.exp(delta[..., None] * A)
            bx = delta[..., None] * Bm[:, :, None, :] * x[..., None]
            dA_t = jnp.transpose(dA, (1, 0, 2, 3))
            bx_t = jnp.transpose(bx, (1, 0, 2, 3))
            c_t = jnp.transpose(Cm, (1, 0, 2))
            h0 = jnp.zeros((x.shape[0], ED, N), dtype=x.dtype)

            def step(h, inp):
                dAi, bxi, ci = inp
                h = dAi * h + bxi
                return (h, jnp.einsum('ben,bn->be', h, ci))
            _, ys = jax.lax.scan(step, h0, (dA_t, bx_t, c_t))
            y = jnp.transpose(ys, (1, 0, 2)) + Dp * x
            return y * jax.nn.silu(z)

        def _mamba_block(x, W_in, conv_w, conv_b, Wx, Wdt, b_dt, A_log, Dp, conv_w_b, conv_b_b, Wx_b, Wdt_b, b_dt_b, A_log_b, Dp_b, W_out):
            xz = x @ W_in.T
            xf, zf = (xz[..., :ED], xz[..., ED:])
            y = _ssm_branch(xf, zf, conv_w, conv_b, Wx, Wdt, b_dt, A_log, Dp)
            xz_r = xz[:, ::-1, :]
            xb, zb = (xz_r[..., :ED], xz_r[..., ED:])
            y_b = _ssm_branch(xb, zb, conv_w_b, conv_b_b, Wx_b, Wdt_b, b_dt_b, A_log_b, Dp_b)
            y = (y + y_b[:, ::-1, :]) * 0.5
            return y @ W_out.T
        return _mamba_block(x, W_in, conv_w, conv_b, Wx, Wdt, b_dt, A_log, Dp, conv_w_b, conv_b_b, Wx_b, Wdt_b, b_dt_b, A_log_b, Dp_b, W_out)

    def _L0_ffn_ref(hidden, router_w, router_b, sw1, sb1, sw2, sb2, rw1, rb1, rw2, rb2):
        import jax, jax.numpy as jnp
        import numpy as np
        D = 256
        H = 512
        E = 8
        TOP_K = 2
        N_SHARED = 1
        B, S = (2, 256)
        b, s, d = hidden.shape
        T = b * s
        flat = hidden.reshape(T, d)
        router_logits = flat @ router_w + router_b
        router_probs = jax.nn.softmax(router_logits, axis=-1)
        topk_probs, topk_idx = jax.lax.top_k(router_probs, TOP_K)
        weights = jnp.zeros_like(router_probs).at[jnp.arange(T)[:, None], topk_idx].add(topk_probs)
        sh = jax.nn.gelu(flat @ sw1 + sb1, approximate=False)
        shared_out = (sh @ sw2 + sb2) / N_SHARED
        h1 = jax.nn.gelu(jnp.einsum('td,edh->teh', flat, rw1) + rb1[None], approximate=False)
        expert_out = jnp.einsum('teh,ehd->ted', h1, rw2) + rb2[None]
        mixed = jnp.einsum('ted,te->td', expert_out, weights)
        return (shared_out + mixed).reshape(b, s, d)
    x = L0_attn_x
    x = x + _layernorm(_L0_attn_ref(_layernorm(x, axis=-1), L0_attn_W_in, L0_attn_conv_w, L0_attn_conv_b, L0_attn_Wx, L0_attn_Wdt, L0_attn_b_dt, L0_attn_A_log, L0_attn_Dp, L0_attn_conv_w_b, L0_attn_conv_b_b, L0_attn_Wx_b, L0_attn_Wdt_b, L0_attn_b_dt_b, L0_attn_A_log_b, L0_attn_Dp_b, L0_attn_W_out), axis=-1)
    x = x + _layernorm(_L0_ffn_ref(_layernorm(x, axis=-1), L0_ffn_router_w, L0_ffn_router_b, L0_ffn_sw1, L0_ffn_sb1, L0_ffn_sw2, L0_ffn_sb2, L0_ffn_rw1, L0_ffn_rb1, L0_ffn_rw2, L0_ffn_rb2), axis=-1)
    return x

_drawn_inputs = setup_inputs


def setup_inputs(seed=0):
    import zlib

    import numpy as np

    out = dict(_drawn_inputs(seed))
    spreads = {'L0_attn_Dp': (1.0, 0.2),
     'L0_attn_Dp_b': (1.0, 0.2),
     'L0_ffn_router_b': (0.0, 0.1),
     'L0_ffn_sb1': (0.0, 0.1),
     'L0_ffn_sb2': (0.0, 0.1),
     'L0_ffn_rb1': (0.0, 0.296),
     'L0_ffn_rb2': (0.0, 0.1)}
    factors = {'L0_attn_conv_b': 4.337,
     'L0_attn_Wdt': 3.019,
     'L0_attn_conv_b_b': 3.928,
     'L0_attn_Wdt_b': 3.069}
    for name, (base, spread) in spreads.items():
        noise = np.random.default_rng([zlib.crc32(name.encode()), seed]).standard_normal(out[name].shape)
        drawn = base * np.exp(spread * noise) if base else spread * noise
        out[name] = jnp.asarray(drawn.astype(out[name].dtype))
    for name, factor in factors.items():
        out[name] = (out[name] * factor).astype(out[name].dtype)
    return out
```

```python
from contextlib import ExitStack

import concourse.bass as bass
from concourse import mybir

F32 = mybir.dt.float32
ALU = mybir.AluOpType
ACT = mybir.ActivationFunctionType
AX_X = mybir.AxisListType.X

P = 128
BANK = 512
TAPS = 4
EPS = 1e-5
TOP_K = 2
CHAN_CONV_W, CHAN_CONV_B, CHAN_B_DT, CHAN_D, CHAN_A = 0, 4, 5, 6, 7


class Mark:

    def __init__(self, nc, ctx, name, step=1):
        self.sem = ctx.enter_context(nc.semaphore(name))
        self.step = step
        self.count = 0

    def on(self, instruction):
        self.count += self.step
        instruction.then_inc(self.sem, self.step)
        return (self, self.count)


class Lane:

    def __init__(self, engine):
        self.e = engine
        self.seen = {}

    def need(self, *marks):
        for m in marks:
            if m is None:
                continue
            mark, count = m
            if self.seen.get(mark, 0) < count:
                self.e.wait_ge(mark.sem, count)
                self.seen[mark] = count


def mamba_moe(nc, x, w_in_t, chan, wx_t, wdt_t, w_out_t, router_w, router_b, w1, b1_t, w2, b2, out):
    NB, L, D = x.shape
    ED = w_out_t.shape[0]
    DTR = wdt_t.shape[1]
    NP = wx_t.shape[2]
    N = (NP - DTR) // 2
    NX = w1.shape[0]
    E = router_w.shape[1]
    H = w1.shape[2]
    NCH = chan.shape[1] // 2
    DC, EC, HC, TB, NH = D // P, ED // P, H // P, L // P, L // BANK
    QB = BANK // P
    assert ED == BANK and H == BANK and L % BANK == 0 and D % P == 0
    PAD = TAPS
    XZW = L + 2 * PAD
    UNITS = N * EC
    NW = 2 * NB
    LOOKAHEAD = 2
    JIT_LEAD = 3

    ctx = ExitStack()
    with ctx:
        def sb(name, shape):
            return ctx.enter_context(nc.sbuf_tensor(name, shape, F32))

        def mark(name, step=1):
            return Mark(nc, ctx, name, step)

        w_in_sb = sb("w_in_sb", [P, DC, 2 * ED])
        wx_sb = sb("wx_sb", [P, 2, EC, NP])
        wdt_sb = sb("wdt_sb", [DTR, 2, ED])
        w_out_sb = sb("w_out_sb", [P, EC, D])
        chan_sb = sb("chan_sb", [P, EC, 2 * NCH])
        neg_a = sb("neg_a", [P, EC, 2, N])
        diag_d = sb("diag_d", [P, 2, EC, P])
        ident = sb("ident", [P, P])
        router_sb = sb("router_sb", [P, DC, E])
        router_b_sb = sb("router_b_sb", [P, E])
        b1_sb = sb("b1_sb", [P, HC, NX])
        b2_sb = sb("b2_sb", [NX, D])
        rank = sb("rank", [P, TB, E])
        minus_half = sb("minus_half", [P, TB])
        expert_w = sb("expert_w", [P, 3, DC * H])

        xu = sb("xu", [P, 2, EC, L])
        delta = sb("delta", [P, EC, L])
        sp_tmp = sb("sp_tmp", [P, L])
        h = sb("h", [P, 2, EC, L])
        b_row = sb("b_row", [P, 2, L])
        drive = sb("drive", [P, 2, L])
        y = sb("y", [P, TB, ED])
        xn_t = sb("xn_t", [P, DC, L])
        dbc = sb("dbc", [NP, L])
        c_col = sb("c_col", [P, 2, TB, N])
        xn2_t = sb("xn2_t", [P, DC, L])
        acc = sb("acc", [P, TB, D])
        work = sb("work", [P, QB * ED + 7 * ED])
        stats = sb("stats", [P, TB, 6])
        mv = sb("mv", [P, TB, 2])
        rstd = sb("rstd", [P, TB])
        logits = sb("logits", [P, TB, E])
        sel1 = sb("sel1", [P, TB, E])
        sel2 = sb("sel2", [P, TB, E])
        cand = sb("cand", [P, TB, E])
        peak = sb("peak", [P, TB])
        mix = sb("mix", [P, TB, NX])

        tokens = work[:, 0:TB * D].rearrange("p (b d) -> p b d", b=TB)
        xz_pad = work[:, TB * D:TB * D + 2 * XZW].rearrange("p (s t) -> p s t", s=2)
        dx_stage = work[:, TB * D + 2 * XZW:TB * D + 2 * XZW + 2 * ED].rearrange("p (s e) -> p s e", s=2)
        z_quad = work[:, 0:QB * ED].rearrange("p (b e) -> p b e", b=QB)
        g_tile = work[:, QB * ED:QB * ED + 6 * ED].rearrange("p (s k e) -> p s k e", s=2, k=3)
        yg_t = work[:, QB * ED + 6 * ED:QB * ED + 7 * ED].rearrange("p (c t) -> p c t", c=EC)
        h1 = work[:, 0:2 * HC * BANK].rearrange("p (g m t) -> p g m t", g=2, m=HC)
        mix_t = work[0:NX, 2 * HC * BANK:2 * HC * BANK + L]

        decay = [ctx.enter_context(nc.psum_tensor(f"decay{i}", [P, L], F32)) for i in range(2)]
        h_t = [ctx.enter_context(nc.psum_tensor(f"h_t{i}", [P, ED], F32)) for i in range(2)]
        side = [ctx.enter_context(nc.psum_tensor(f"side{i}", [P, BANK], F32)) for i in range(2)]

        b_dram = nc.dram_tensor("b_dram", [2, N, L], F32, kind="Internal").ap()
        xn_dram = nc.dram_tensor("xn_dram", [2, P, DC * L], F32, kind="Internal").ap()
        dx_dram = nc.dram_tensor("dx_dram", [2, 2, L, ED], F32, kind="Internal").ap()
        y_dram = nc.dram_tensor("y_dram", [L, ED], F32, kind="Internal").ap()
        x1_dram = nc.dram_tensor("x1_dram", [P, TB * D], F32, kind="Internal").ap()

        pe, dve, act, pool, sp = (Lane(e) for e in (nc.tensor, nc.vector, nc.scalar, nc.gpsimd, nc.sync))

        m_const = mark("m_const", 16)
        m_ident = mark("m_ident")
        m_neg_a = mark("m_neg_a")
        m_setup = mark("m_setup")
        m_setup_pool = mark("m_setup_pool")
        m_decay = mark("m_decay")
        m_drive = mark("m_drive")
        m_scan = mark("m_scan")
        m_turn = mark("m_turn")
        m_y = mark("m_y")
        m_dt_mm = mark("m_dt_mm")
        m_dt_act = mark("m_dt_act")
        m_delta = mark("m_delta")
        m_u = mark("m_u")
        m_brow = [mark(f"m_brow{i}", 16) for i in range(2)]
        m_bdram = mark("m_bdram", 16)
        m_ydump = [mark(f"m_ydump{i}", 16) for i in range(TB)]
        m_side_mm = mark("m_side_mm")
        m_side_act = mark("m_side_act")
        m_side_dve = mark("m_side_dve")
        m_side_pool = mark("m_side_pool")
        m_tok = mark("m_tok", 16)
        m_xnst = mark("m_xnst", 16)
        m_xnld = mark("m_xnld", 16)
        m_dxst = [mark(f"m_dxst{i}", 16) for i in range(2)]
        m_gld = [[mark(f"m_gld{i}{k}", 16) for k in range(3)] for i in range(2)]
        m_x1st = mark("m_x1st", 16)
        m_x1ld = mark("m_x1ld", 16)
        m_ew = [mark(f"m_ew{i}", 16) for i in range(3)]
        m_out = mark("m_out", 16)

        loads = [
            (w_in_sb[:, :, :], w_in_t.rearrange("(c p) e -> p c e", p=P)),
            (chan_sb[:, :, :], chan.rearrange("(c p) k -> p c k", p=P)),
            (wx_sb[:, 0, :, :], wx_t[0].rearrange("(c p) k -> p c k", p=P)),
            (wx_sb[:, 1, :, :], wx_t[1].rearrange("(c p) k -> p c k", p=P)),
            (wdt_sb[:, 0, :], wdt_t[0]),
            (wdt_sb[:, 1, :], wdt_t[1]),
            (w_out_sb[:, :, :], w_out_t.rearrange("(c p) d -> p c d", p=P)),
            (router_sb[:, :, :], router_w.rearrange("(c p) e -> p c e", p=P)),
            (router_b_sb[:, :], router_b.rearrange("(a e) -> a e", a=1).to_broadcast([P, E])),
            (b1_sb[:, :, :], b1_t.rearrange("(m p) x -> p m x", p=P)),
            (b2_sb[:, :], b2),
        ]
        for dst, src in loads:
            consts = m_const.on(sp.e.dma_start(dst, src))

        pool.need(m_ident.on(pool.e.memset(ident[:, :], 0.0)))
        ident_ready = m_ident.on(pool.e.affine_select(
            out=ident[:, :], in_=ident[:, :], compare_op=ALU.not_equal, fill=1.0, base=0,
            pattern=[[-1, P]], channel_multiplier=1))
        half_ready = m_setup_pool.on(pool.e.memset(minus_half[:, :], -0.5))
        for e in range(E):
            rank_ready = m_setup_pool.on(pool.e.memset(rank[:, :, e:e + 1], float(E - e)))
        ones_ready = m_setup_pool.on(pool.e.memset(mix[:, :, E:NX], 1.0))

        dve.need(consts, ident_ready)
        for d in range(2):
            for c in range(EC):
                k = d * NCH + CHAN_D
                diag_ready = m_setup.on(dve.e.tensor_scalar(
                    diag_d[:, d, c, :], ident[:, :], chan_sb[:, c, k:k + 1], None, ALU.mult))
        act.e.preload_act_table_set("natural_log_exp_and_others")
        act.need(consts)
        for d in range(2):
            k = d * NCH + CHAN_A
            ea = m_neg_a.on(act.e.activation(neg_a[:, :, d, :], chan_sb[:, :, k:k + N], ACT.Exp))
        act.need(ea)
        neg_a_ready = m_neg_a.on(act.e.mul(neg_a[:, :, :, :], neg_a[:, :, :, :], -1.0))

        def chan_col(d, c, k):
            return chan_sb[:, c, d * NCH + k:d * NCH + k + 1]

        bank_free = [None, None]
        bank_held = [False, False]
        bank_next = [0]

        def take_bank():
            i = bank_next[0] % 2
            if bank_held[i]:
                i = 1 - i
            assert not bank_held[i]
            bank_next[0] = i + 1
            bank_held[i] = True
            pe.need(bank_free[i])
            return i

        def give_bank(i, token):
            bank_free[i] = token
            bank_held[i] = False

        def products(dst, pairs, m):
            for i, (lhs, rhs) in enumerate(pairs):
                last = pe.e.matmul(dst, lhs, rhs, start=(i == 0), stop=(i == len(pairs) - 1))
            return m.on(last)

        def turns(items, m):
            for dst, src in items:
                k = src.shape[0]
                last = pe.e.transpose(dst, src, ident[0:k, 0:k])
            return m.on(last)

        decay_done, drive_done, scan_done = {}, {}, {}
        turn_done, y_done = {}, {}
        delta_ready, u_ready, x_ready, x_read = {}, {}, {}, {}
        dbc_ready, dbc_read, c_ready, b_stored, b_row_ready = {}, {}, {}, {}, {}
        y_dumped, y_loaded = {}, {}
        xn_ready, xn_stored, xn_loaded = {}, {}, {}
        dx_stored, dx_loaded = {}, {}
        xn_t_read = [None]
        work_read = []
        acc_read = [None]
        xn2_read = [None]
        x1_loaded = [None]
        x1_stored = [None]
        mix_read = [None]

        def hand_over(*marks):
            work_read[:] = [m for m in marks if m is not None]

        def start_window_chunk(w, c):
            b, d = divmod(w, 2)
            prev_last = (w * UNITS) - EC + c
            for s in range(NH):
                i = take_bank()
                pe.need(dbc_ready[w])
                mm = products(side[i][:, :], [(wdt_sb[:, d, c * P:(c + 1) * P],
                                               dbc[0:DTR, s * BANK:(s + 1) * BANK])], m_dt_mm)
                act.need(mm, decay_done.get(prev_last))
                pre = m_dt_act.on(act.e.activation(delta[:, c, s * BANK:(s + 1) * BANK], side[i][:, :],
                                                   ACT.Identity, bias=chan_col(d, c, CHAN_B_DT)))
                give_bank(i, pre)
            dbc_read[w] = mm
            act.need(pre, delta_ready.get("tmp"))
            tmp = m_dt_act.on(act.e.activation(sp_tmp[:, :], delta[:, c, :], ACT.Abs))
            act.need(tmp)
            tmp = m_dt_act.on(act.e.activation(sp_tmp[:, :], sp_tmp[:, :], ACT.Exp, scale=-1.0))
            act.need(tmp)
            tmp = m_dt_act.on(act.e.activation(sp_tmp[:, :], sp_tmp[:, :], ACT.Ln, bias=1.0))
            dve.need(tmp)
            delta_ready[w, c] = delta_ready["tmp"] = m_delta.on(dve.e.scalar_tensor_tensor(
                out=delta[:, c, :], in0=delta[:, c, :], scalar=0.0, in1=sp_tmp[:, :],
                op0=ALU.max, op1=ALU.add))
            pool.need(delta_ready[w, c], x_ready[w], x_read[w])
            u_ready[w, c] = m_u.on(pool.e.tensor_tensor(xu[:, d, c, :], xu[:, d, c, :], delta[:, c, :], ALU.mult))

        def load_b_row(gn):
            w, n = divmod(gn, N)
            sp.need(b_stored[w], drive_done.get((gn - 2) * EC + EC - 1))
            b_row_ready[gn] = m_brow[gn % 2].on(sp.e.dma_start(
                b_row[:, gn % 2, :], b_dram[w % 2, n:n + 1, :].to_broadcast([P, L])))

        def feed_unit(k):
            gn, c = divmod(k, EC)
            w, n = divmod(gn, N)
            d = w % 2
            act.need(neg_a_ready, delta_ready[w, c], scan_done.get(k - 2))
            decay_done[k] = m_decay.on(act.e.activation(decay[k % 2][:, :], delta[:, c, :], ACT.Exp,
                                                        scale=neg_a[:, c, d, n:n + 1]))
            pool.need(u_ready[w, c], b_row_ready[gn], scan_done.get(k - 2))
            drive_done[k] = m_drive.on(pool.e.tensor_tensor(drive[:, k % 2, :], xu[:, d, c, :],
                                                            b_row[:, gn % 2, :], ALU.mult))

        def scan_unit(k):
            gn, c = divmod(k, EC)
            d = (gn // N) % 2
            dve.need(decay_done[k], drive_done[k], turn_done.get((gn - 2) * TB + TB - 1))
            o, a, v = h[:, gn % 2, c, :], decay[k % 2][:, :], drive[:, k % 2, :]
            if d:
                o, a, v = h[:, gn % 2, c, ::-1], decay[k % 2][:, ::-1], drive[:, k % 2, ::-1]
            scan_done[k] = m_scan.on(dve.e.tensor_tensor_scan(o, a, v, 0.0, ALU.mult, ALU.add))

        def turn_tile(i):
            gn, tb = divmod(i, TB)
            pe.need(ident_ready, scan_done[gn * EC + EC - 1], y_done.get(i - 2))
            turn_done[i] = turns([(h_t[i % 2][:, c * P:(c + 1) * P],
                                   h[:, gn % 2, c, tb * P:(tb + 1) * P]) for c in range(EC)], m_turn)

        def sum_tile(i):
            gn, tb = divmod(i, TB)
            w, n = divmod(gn, N)
            b, d = divmod(w, 2)
            c_n = c_col[:, w % 2, tb, n:n + 1]
            if d == 0 and n == 0:
                dve.need(turn_done[i], c_ready[w], y_dumped.get((b - 1, tb)))
                y_done[i] = m_y.on(dve.e.tensor_scalar(y[:, tb, :], h_t[i % 2][:, :], c_n, None, ALU.mult))
            else:
                dve.need(turn_done[i], c_ready[w], y_done[i - TB])
                y_done[i] = m_y.on(dve.e.scalar_tensor_tensor(
                    out=y[:, tb, :], in0=h_t[i % 2][:, :], scalar=c_n, in1=y[:, tb, :],
                    op0=ALU.mult, op1=ALU.add))
            if d == 1 and n == N - 1:
                sp.need(y_done[i], y_loaded.get((b - 1, tb)))
                y_dumped[b, tb] = m_ydump[tb].on(sp.e.dma_start(y_dram[tb * P:(tb + 1) * P, :], y[:, tb, :]))

        def norm_tokens(src, dst, token):
            dve.need(token, norm_free[0])
            for tb in range(TB):
                st = m_side_dve.on(dve.e.bn_stats(stats[:, tb, :], src[:, tb, :]))
            yield 0.0
            dve.need(st)
            for tb in range(TB):
                st = m_side_dve.on(dve.e.bn_aggr(mv[:, tb, :], stats[:, tb, :]))
            dve.need(st)
            st = m_side_dve.on(dve.e.tensor_scalar(rstd[:, :], mv[:, :, 1], EPS, None, ALU.add))
            pool.need(st, half_ready)
            r = m_side_pool.on(pool.e.tensor_tensor(rstd[:, :], rstd[:, :], minus_half[:, :], ALU.pow))
            yield 0.0
            yield 0.0
            dve.need(r)
            for tb in range(TB):
                st = m_side_dve.on(dve.e.tensor_scalar(dst[:, tb, :], src[:, tb, :], mv[:, tb, 0:1],
                                                       rstd[:, tb:tb + 1], ALU.subtract, ALU.mult))
                if tb == TB // 2:
                    yield 0.0
            norm_free[0] = st
            normed[0] = st

        norm_free, normed = [None], [None]

        def turn_tokens(src, dst, token, dst_free):
            pe.need(token, ident_ready)
            for c in range(DC):
                for s in range(NH):
                    i = take_bank()
                    t = turns([(side[i][:, q * P:(q + 1) * P], src[:, s * QB + q, c * P:(c + 1) * P])
                               for q in range(QB)], m_side_mm)
                    yield 0.5
                    act.need(t, dst_free)
                    e = m_side_act.on(act.e.copy(dst[:, c, s * BANK:(s + 1) * BANK], side[i][:, :]))
                    give_bank(i, e)
            turned[0] = (t, e)

        turned = [None]

        def prepare(w):
            b, d = divmod(w, 2)
            busy = tuple(work_read)
            if d == 0:
                sp.need(*busy)
                t = m_tok.on(sp.e.dma_start(tokens[:, :, :], x[b].rearrange("(b p) d -> p b d", p=P)))
                yield 0.0
                yield from norm_tokens(tokens, tokens, t)
                yield from turn_tokens(tokens, xn_t, normed[0], xn_t_read[0])
                tokens_turned, xn_ready[b] = turned[0]
                sp.need(xn_ready[b], xn_loaded.get(b - 2))
                xn_stored[b] = m_xnst.on(sp.e.dma_start(xn_dram[b % 2], xn_t[:, :, :].rearrange("p c t -> p (c t)")))
            pool.need(*busy)
            pool.e.memset(xz_pad[:, :, 0:PAD], 0.0)
            pads = m_side_pool.on(pool.e.memset(xz_pad[:, :, PAD + L:XZW], 0.0))
            xz_read = [None, None]
            buffer_free = drive_done.get((w - 1) * UNITS - 1)
            pe.need(consts)
            for c in range(EC):
                zb = xz_pad[:, c % 2, :]
                for s in range(NH):
                    i = take_bank()
                    pe.need(xn_ready[b])
                    mm = products(side[i][:, :], [(w_in_sb[:, k, c * P:(c + 1) * P],
                                                   xn_t[:, k, s * BANK:(s + 1) * BANK]) for k in range(DC)], m_side_mm)
                    yield 1.8
                    act.need(mm, xz_read[c % 2], *busy)
                    xz = m_side_act.on(act.e.copy(zb[:, PAD + s * BANK:PAD + (s + 1) * BANK], side[i][:, :]))
                    give_bank(i, xz)
                dve.need(xz, pads, buffer_free)
                starts = [PAD + (TAPS - 1 - k) * (1 if d else -1) for k in range(TAPS)]
                v = m_side_dve.on(dve.e.tensor_scalar(
                    xu[:, d, c, :], zb[:, starts[0]:starts[0] + L], chan_col(d, c, CHAN_CONV_W),
                    chan_col(d, c, CHAN_CONV_B), ALU.mult, ALU.add))
                for k in range(1, TAPS):
                    yield 0.0
                    dve.need(v)
                    v = m_side_dve.on(dve.e.scalar_tensor_tensor(
                        out=xu[:, d, c, :], in0=zb[:, starts[k]:starts[k] + L],
                        scalar=chan_col(d, c, CHAN_CONV_W + k), in1=xu[:, d, c, :], op0=ALU.mult, op1=ALU.add))
                xz_read[c % 2] = v
            if d == 1:
                xn_t_read[0] = mm
            yield 0.0
            act.need(v)
            x_ready[w] = m_side_act.on(act.e.activation(xu[:, d, :, :], xu[:, d, :, :], ACT.Silu))
            act.e.preload_act_table_set("natural_log_exp_and_others")
            yield 0.0
            for s in range(NH):
                i = take_bank()
                pe.need(x_ready[w])
                mm = products(side[i][0:NP, :], [(wx_sb[:, d, c, :], xu[:, d, c, s * BANK:(s + 1) * BANK])
                                                 for c in range(EC)], m_side_mm)
                yield 3.6
                act.need(mm, dbc_read.get(w - 1), b_stored.get(w - 1), c_ready.get(w - 1))
                dbc_ready[w] = m_side_act.on(act.e.copy(dbc[:, s * BANK:(s + 1) * BANK], side[i][0:NP, :]))
                give_bank(i, dbc_ready[w])
            sp.need(dbc_ready[w], b_row_ready.get((w - 1) * N - 1), b_row_ready.get((w - 1) * N - 2))
            b_stored[w] = m_bdram.on(sp.e.dma_start(b_dram[w % 2], dbc[DTR:DTR + N, :]))
            for s in range(NH):
                i = take_bank()
                pe.need(dbc_ready[w], ident_ready)
                t = turns([(side[i][:, q * NP:(q + 1) * NP], dbc[:, (s * QB + q) * P:(s * QB + q + 1) * P])
                           for q in range(QB)], m_side_mm)
                yield 0.5
                act.need(t, y_done.get((w - 1) * N * TB - 1))
                c_ready[w] = m_side_act.on(act.e.copy(
                    c_col[:, w % 2, s * QB:(s + 1) * QB, :],
                    side[i][:, 0:QB * NP].rearrange("p (q k) -> p q k", q=QB)[:, :, DTR + N:NP]))
                give_bank(i, c_ready[w])
            for tb in range(TB):
                i = take_bank()
                pe.need(diag_ready)
                for c in range(EC):
                    mm = pe.e.matmul(side[i][:, c * P:(c + 1) * P], xu[:, d, c, tb * P:(tb + 1) * P],
                                     diag_d[:, d, c, :], start=True, stop=True)
                mm = m_side_mm.on(mm)
                yield 1.0
                act.need(mm, dx_stored.get("stage", {}).get(tb % 2), *busy)
                e = m_side_act.on(act.e.copy(dx_stage[:, tb % 2, :], side[i][:, :]))
                give_bank(i, e)
                sp.need(e, dx_loaded.get((b - 2, d, tb)))
                dx_stored[w, tb] = m_dxst[tb % 2].on(sp.e.dma_start(
                    dx_dram[b % 2, d, tb * P:(tb + 1) * P, :], dx_stage[:, tb % 2, :]))
                dx_stored.setdefault("stage", {})[tb % 2] = dx_stored[w, tb]
            x_read[w] = mm
            hand_over(v, e, dx_stored[w, TB - 1], dx_stored[w, TB - 2], *([tokens_turned] if d == 0 else []))

        def gate(b):
            busy = tuple(work_read)
            sp.need(xn_t_read[0], xn_stored[b])
            xn_loaded[b] = m_xnld.on(sp.e.dma_start(xn_t[:, :, :].rearrange("p c t -> p (c t)"), xn_dram[b % 2]))
            tile_read = [None, None]
            yg_read = None
            z_read = None

            def load_tiles(tb):
                rows = slice(tb * P, (tb + 1) * P)
                sources = [(y_dram[rows, :], y_dumped[b, tb]),
                           (dx_dram[b % 2, 0, rows, :], dx_stored[2 * b, tb]),
                           (dx_dram[b % 2, 1, rows, :], dx_stored[2 * b + 1, tb])]
                for k, (src, stored) in enumerate(sources):
                    sp.need(stored, tile_read[tb % 2], *busy)
                    got[tb, k] = m_gld[tb % 2][k].on(sp.e.dma_start(g_tile[:, tb % 2, k, :], src))
                y_loaded[b, tb] = got[tb, 0]
                dx_loaded[b, 0, tb] = got[tb, 1]
                dx_loaded[b, 1, tb] = got[tb, 2]

            got = {}
            load_tiles(0)
            yield 0.0
            for quad in range(TB // QB):
                for q in range(QB):
                    tb = quad * QB + q
                    i = take_bank()
                    pe.need(xn_loaded[b])
                    mm = products(side[i][:, :], [(xn_t[:, k, tb * P:(tb + 1) * P], w_in_sb[:, k, ED:2 * ED])
                                                  for k in range(DC)], m_side_mm)
                    yield 1.8
                    act.need(mm, z_read, *busy)
                    z = m_side_act.on(act.e.copy(z_quad[:, q, :], side[i][:, :]))
                    give_bank(i, z)
                act.need(z)
                z = m_side_act.on(act.e.activation(z_quad[:, :, :], z_quad[:, :, :], ACT.Silu))
                act.e.preload_act_table_set("natural_log_exp_and_others")
                for q in range(QB):
                    tb = quad * QB + q
                    if tb + 1 < TB:
                        load_tiles(tb + 1)
                    t = g_tile[:, tb % 2, :, :]
                    pool.need(got[tb, 0], got[tb, 1])
                    v = m_side_pool.on(pool.e.tensor_tensor(t[:, 0, :], t[:, 0, :], t[:, 1, :], ALU.add))
                    pool.need(got[tb, 2], v)
                    v = m_side_pool.on(pool.e.tensor_tensor(t[:, 0, :], t[:, 0, :], t[:, 2, :], ALU.add))
                    pool.need(z, v)
                    z_read = m_side_pool.on(pool.e.tensor_tensor(t[:, 0, :], t[:, 0, :], z_quad[:, q, :], ALU.mult))
                    yield 0.0
                    yield 0.0
                    i = take_bank()
                    pe.need(z_read)
                    tile_read[tb % 2] = turns([(side[i][:, c * P:(c + 1) * P], t[:, 0, c * P:(c + 1) * P])
                                               for c in range(EC)], m_side_mm)
                    yield 0.5
                    act.need(tile_read[tb % 2], yg_read)
                    e = m_side_act.on(act.e.copy(yg_t[:, :, :].rearrange("p c t -> p (c t)"), side[i][:, :]))
                    give_bank(i, e)
                    yield 0.0
                    i = take_bank()
                    pe.need(e)
                    yg_read = products(side[i][:, 0:D], [(yg_t[:, c, :], w_out_sb[:, c, :]) for c in range(EC)], m_side_mm)
                    yield 1.8
                    act.need(yg_read, acc_read[0])
                    o = m_side_act.on(act.e.mul(acc[:, tb, :], side[i][:, 0:D], 0.5))
                    give_bank(i, o)
            xn_t_read[0] = mm
            sp.need(z_read)
            t = m_tok.on(sp.e.dma_start(tokens[:, :, :], x[b].rearrange("(b p) d -> p b d", p=P)))
            yield from norm_tokens(acc, acc, o)
            dve.need(normed[0], t)
            r = m_side_dve.on(dve.e.tensor_tensor(acc[:, :, :], acc[:, :, :], tokens[:, :, :], ALU.add))
            sp.need(r, x1_loaded[0])
            x1_stored[0] = m_x1st.on(sp.e.dma_start(x1_dram, acc[:, :, :].rearrange("p b d -> p (b d)")))
            yield 0.0
            yield from norm_tokens(acc, tokens, r)
            yield from turn_tokens(tokens, xn2_t, normed[0], xn2_read[0])
            tokens_turned, xn2_ready[0] = turned[0]
            hand_over(tokens_turned)

        xn2_ready = [None]

        def route(b):
            busy = tuple(work_read)
            i = take_bank()
            pe.need(xn2_ready[0])
            for tb in range(TB):
                lg = products(side[i][:, tb * E:(tb + 1) * E],
                              [(xn2_t[:, k, tb * P:(tb + 1) * P], router_sb[:, k, :]) for k in range(DC)], m_side_mm)
            yield 1.5
            dve.need(lg)
            v = m_side_dve.on(dve.e.tensor_tensor(
                logits[:, :, :], side[i][:, 0:TB * E].rearrange("p (b e) -> p b e", b=TB),
                router_b_sb[:, :].rearrange("p (a e) -> p a e", a=1).to_broadcast([P, TB, E]), ALU.add))
            give_bank(i, v)

            def step(instruction):
                v = m_side_dve.on(instruction)
                dve.need(v)
                return v

            def wide():
                return peak[:, :].rearrange("p (b a) -> p b a", a=1).to_broadcast([P, TB, E])

            dve.need(v)
            step(dve.e.tensor_reduce(peak[:, :], logits[:, :, :], AX_X, ALU.max))
            v = step(dve.e.tensor_tensor(logits[:, :, :], logits[:, :, :], wide(), ALU.subtract))
            act.need(v)
            v = m_side_act.on(act.e.activation(logits[:, :, :], logits[:, :, :], ACT.Exp))
            yield 0.0
            yield 0.0
            dve.need(v)
            step(dve.e.tensor_reduce(peak[:, :], logits[:, :, :], AX_X, ALU.add))
            step(dve.e.reciprocal(peak[:, :], peak[:, :]))
            step(dve.e.tensor_tensor(logits[:, :, :], logits[:, :, :], wide(), ALU.mult))
            dve.need(rank_ready, ones_ready, mix_read[0])

            def first_of_largest(p, sel):
                step(dve.e.tensor_reduce(peak[:, :], p, AX_X, ALU.max))
                step(dve.e.tensor_tensor(cand[:, :, :], p, wide(), ALU.is_equal))
                step(dve.e.tensor_tensor(cand[:, :, :], cand[:, :, :], rank[:, :, :], ALU.mult))
                step(dve.e.tensor_reduce(peak[:, :], cand[:, :, :], AX_X, ALU.max))
                step(dve.e.tensor_tensor(sel, cand[:, :, :], wide(), ALU.is_equal))

            first_of_largest(logits[:, :, :], sel1[:, :, :])
            yield 0.0
            step(dve.e.scalar_tensor_tensor(out=mix[:, :, 0:E], in0=sel1[:, :, :], scalar=-2.0,
                                            in1=logits[:, :, :], op0=ALU.mult, op1=ALU.add))
            first_of_largest(mix[:, :, 0:E], sel2[:, :, :])
            step(dve.e.tensor_tensor(sel1[:, :, :], sel1[:, :, :], sel2[:, :, :], ALU.add))
            mixed = step(dve.e.tensor_tensor(mix[:, :, 0:E], logits[:, :, :], sel1[:, :, :], ALU.mult))
            yield 0.0
            for s in range(NH):
                i = take_bank()
                pe.need(mixed)
                t = turns([(side[i][0:NX, q * P:(q + 1) * P], mix[:, s * QB + q, :]) for q in range(QB)], m_side_mm)
                yield 0.5
                act.need(t, *busy)
                mt = m_side_act.on(act.e.copy(mix_t[:, s * BANK:(s + 1) * BANK], side[i][0:NX, :]))
                give_bank(i, mt)
            for tb in range(TB):
                i = take_bank()
                pe.need(mt, x1_stored[0])
                mm = products(side[i][:, 0:D], [(mix_t[:, tb * P:(tb + 1) * P], b2_sb[:, :])], m_side_mm)
                yield 0.6
                act.need(mm, x1_stored[0])
                acc_done[tb] = m_side_act.on(act.e.copy(acc[:, tb, :], side[i][:, 0:D]))
                give_bank(i, acc_done[tb])
            hand_over(*busy, mm)

        acc_done = {}
        expert_loaded, expert_read = {}, {}

        def load_expert(s):
            if s >= 2 * NX * NB or s in expert_loaded:
                return
            xp, k = divmod(s % (2 * NX), 2)
            src = w1[xp].rearrange("(c p) n -> p c n", p=P) if k == 0 else w2[xp].rearrange("(c p) n -> p c n", p=P)
            sp.need(expert_read.get(s - 3))
            expert_loaded[s] = m_ew[s % 3].on(sp.e.dma_start(
                expert_w[:, s % 3, :].rearrange("p (c n) -> p c n", n=src.shape[2]), src))

        h1_read = [None, None]

        def experts(b, first, last):
            busy = tuple(work_read)
            for xp in range(first, last):
                s = 2 * (b * NX + xp)
                load_expert(s)
                load_expert(s + 1)
                wi = expert_w[:, s % 3, :].rearrange("p (c n) -> p c n", n=H)
                wo = expert_w[:, (s + 1) % 3, :].rearrange("p (c n) -> p c n", n=D)
                hid = [None, None]
                for g in range(NH):
                    for m in range(HC):
                        i = take_bank()
                        pe.need(expert_loaded[s])
                        mm = products(side[i][:, :], [(wi[:, k, m * P:(m + 1) * P],
                                                       xn2_t[:, k, g * BANK:(g + 1) * BANK]) for k in range(DC)], m_side_mm)
                        yield 1.8
                        act.need(mm, h1_read[g], *busy)
                        e = m_side_act.on(act.e.activation(h1[:, g, m, :], side[i][:, :], ACT.Identity,
                                                           bias=b1_sb[:, m, xp:xp + 1]))
                        give_bank(i, e)
                    act.need(e)
                    hid[g] = m_side_act.on(act.e.activation(h1[:, g, :, :], h1[:, g, :, :], ACT.Gelu))
                    act.e.preload_act_table_set("natural_log_exp_and_others")
                expert_read[s] = mm
                load_expert(s + 2)
                for g in range(NH):
                    for q in range(QB):
                        tb = g * QB + q
                        i = take_bank()
                        pe.need(hid[g], expert_loaded[s + 1])
                        mm = products(side[i][:, 0:D], [(h1[:, g, m, q * P:(q + 1) * P], wo[:, m, :])
                                                        for m in range(HC)], m_side_mm)
                        yield 1.8
                        dve.need(mm, acc_done[tb])
                        acc_done[tb] = m_side_dve.on(dve.e.scalar_tensor_tensor(
                            out=acc[:, tb, :], in0=side[i][:, 0:D], scalar=mix[:, tb, xp:xp + 1],
                            in1=acc[:, tb, :], op0=ALU.mult, op1=ALU.add))
                        give_bank(i, acc_done[tb])
                    h1_read[g] = mm
                expert_read[s + 1] = mm
            hand_over(*busy, mm)
            if last == NX:
                xn2_read[0] = mm
                mix_read[0] = acc_done[TB - 1]

        def finish(b):
            busy = tuple(work_read)
            sp.need(x1_stored[0], *busy)
            x1_loaded[0] = m_x1ld.on(sp.e.dma_start(tokens[:, :, :].rearrange("p b d -> p (b d)"), x1_dram))
            yield from norm_tokens(acc, acc, acc_done[TB - 1])
            dve.need(normed[0], x1_loaded[0])
            r = m_side_dve.on(dve.e.tensor_tensor(acc[:, :, :], acc[:, :, :], tokens[:, :, :], ALU.add))
            sp.need(r)
            acc_read[0] = m_out.on(sp.e.dma_start(out[b].rearrange("(b p) d -> p b d", p=P), acc[:, :, :]))
            hand_over(r)

        SPLIT = 4

        def side_work(w):
            b, d = divmod(w, 2)
            if d == 0:
                yield from prepare(w + 1)
                if b > 0:
                    yield from gate(b - 1)
                    yield from route(b - 1)
                    yield from experts(b - 1, 0, SPLIT)
            else:
                if b + 1 < NB:
                    yield from prepare(w + 1)
                if b > 0:
                    yield from experts(b - 1, SPLIT, NX)
                    yield from finish(b - 1)

        def side_cost(w):
            b, d = divmod(w, 2)
            cost = (14.4 + 7.2 + 1 + 8) * (d == 0 or b + 1 < NB)
            if b > 0:
                cost += 14.4 + TB * 2.3 + 8 + SPLIT * 28.8 if d == 0 else (NX - SPLIT) * 28.8
            return max(cost, 150.0)

        for _ in prepare(0):
            pass
        NU = NW * UNITS

        def feed(k):
            if k + JIT_LEAD < NU and (k + JIT_LEAD) % UNITS < EC:
                kj = k + JIT_LEAD
                start_window_chunk(kj // UNITS, kj % UNITS)
            if k % EC == 0 and k + EC < NU:
                load_b_row(k // EC + 1)
            if k < NU:
                feed_unit(k)

        for c in range(JIT_LEAD):
            start_window_chunk(0, c)
        load_b_row(0)
        for k in range(LOOKAHEAD):
            feed(k)
        tile = 0
        for k in range(NU + EC):
            w = k // UNITS
            if k % UNITS == 0 and w < NW:
                work_now = side_work(w)
                rate = side_cost(w) / (2 * (UNITS - EC))
                done = spent = 0.0
            if k < NU:
                scan_unit(k)
                feed(k + LOOKAHEAD)
            for half in range(2):
                if k >= EC:
                    i = 2 * (k - EC) + half
                    if i == 0:
                        turn_tile(0)
                    nxt = i + 1
                    if nxt < (k // EC) * TB if k < NU else nxt < NU * TB // EC:
                        turn_tile(nxt)
                    sum_tile(i)
                    if nxt >= (k // EC) * TB and k < NU and nxt < NU * TB // EC:
                        late_turn = nxt
                        pending_turn = True
                    else:
                        pending_turn = False
                else:
                    pending_turn = False
                if w < NW:
                    done += rate
                    while spent < done or (k % UNITS >= UNITS - EC and half == 1):
                        step = next(work_now, None)
                        if step is None:
                            break
                        spent += step + 0.15
                if pending_turn and (k + 1) % EC == 0:
                    turn_tile(late_turn)
            if w < NW and k % UNITS == UNITS - 1:
                for _ in work_now:
                    pass
        for task in (gate(NB - 1), route(NB - 1), experts(NB - 1, 0, NX), finish(NB - 1)):
            for _ in task:
                pass
        sp.need((m_out, m_out.count), (m_bdram, m_bdram.count), (m_xnst, m_xnst.count), (m_x1st, m_x1st.count),
                *[(m, m.count) for m in m_dxst + m_ydump])


def kernel(**inputs):
    import numpy as np
    import concourse.bacc as bacc
    from concourse.bass_utils import run_bass_kernel_spmd as run

    a = {k: np.asarray(v) for k, v in inputs.items()}

    def chan(s):
        cols = [a["L0_attn_conv_w" + s][:, 0, :], a["L0_attn_conv_b" + s][:, None], a["L0_attn_b_dt" + s][:, None],
                a["L0_attn_Dp" + s][:, None], a["L0_attn_A_log" + s]]
        return np.concatenate(cols, axis=1)

    arrays = {
        "x": a["L0_attn_x"],
        "w_in_t": a["L0_attn_W_in"].T,
        "chan": np.concatenate([chan(""), chan("_b")], axis=1),
        "wx_t": np.stack([a["L0_attn_Wx"].T, a["L0_attn_Wx_b"].T]),
        "wdt_t": np.stack([a["L0_attn_Wdt"].T, a["L0_attn_Wdt_b"].T]),
        "w_out_t": a["L0_attn_W_out"].T,
        "router_w": a["L0_ffn_router_w"],
        "router_b": a["L0_ffn_router_b"],
        "w1": np.concatenate([a["L0_ffn_rw1"], a["L0_ffn_sw1"][None]]),
        "b1_t": np.concatenate([a["L0_ffn_rb1"], a["L0_ffn_sb1"][None]]).T,
        "w2": np.concatenate([a["L0_ffn_rw2"], a["L0_ffn_sw2"][None]]),
        "b2": np.concatenate([a["L0_ffn_rb2"], a["L0_ffn_sb2"][None]]),
    }
    arrays = {f"in_{k}": np.ascontiguousarray(v) for k, v in arrays.items()}
    nc = bacc.Bacc("TRN2", target_bir_lowering=False, num_devices=1)
    args = [nc.dram_tensor(k, v.shape, mybir.dt.from_np(v.dtype), kind="ExternalInput").ap() for k, v in arrays.items()]
    out = nc.dram_tensor("out", a["L0_attn_x"].shape, F32, kind="ExternalOutput").ap()
    mamba_moe(nc, *args, out)
    r = run(nc, [arrays], core_ids=[0])
    return r.results[0]["out"]
```

```python
from contextlib import ExitStack

import concourse.bass as bass
from concourse import mybir

F32 = mybir.dt.float32
ALU = mybir.AluOpType
ACT = mybir.ActivationFunctionType
AX_X = mybir.AxisListType.X

P = 128
BANK = 512
TAPS = 4
EPS = 1e-5
DMA_RING_BYTES = 1024
N_DECAY = 2
N_DRIVE = 2
N_B_ROW = 3
N_H_T = 2
N_SIDE = 6
PACE = 1
LATENCY = 2.0
TAP_COST = 0.6
PREP_COST = (72.6, 100.3)
MIX_COST = 410.5
CHAN_CONV_W, CHAN_CONV_B, CHAN_B_DT, CHAN_D, CHAN_A = 0, 4, 5, 6, 7


class Mark:

    def __init__(self, nc, ctx, name, step=1):
        self.sem = ctx.enter_context(nc.semaphore(name))
        self.step = step
        self.count = 0

    def on(self, instruction):
        self.count += self.step
        instruction.then_inc(self.sem, self.step)
        return (self, self.count)


class Lane:

    def __init__(self, engine):
        self.e = engine
        self.seen = {}

    def need(self, *marks):
        for m in marks:
            if m is None:
                continue
            mark, count = m
            if self.seen.get(mark, 0) < count:
                self.e.wait_ge(mark.sem, count)
                self.seen[mark] = count


def mamba_moe(nc, x, w_in_t, chan, wx_t, wdt_t, w_out_t, router_w, router_b, w1, b1_t, w2, b2, out):
    NB, L, D = x.shape
    ED = w_out_t.shape[0]
    DTR = wdt_t.shape[1]
    NP = wx_t.shape[2]
    N = (NP - DTR) // 2
    NX = w1.shape[0]
    E = router_w.shape[1]
    H = w1.shape[2]
    NCH = chan.shape[1] // 2
    DC, EC, HC, TB, NH = D // P, ED // P, H // P, L // P, L // BANK
    QB = BANK // P
    assert ED == BANK and H == BANK and L % BANK == 0 and D % P == 0
    PAD = TAPS
    XZW = L + 2 * PAD
    UNITS = N * EC
    NW = 2 * NB
    LOOKAHEAD = 2

    ctx = ExitStack()
    with ctx:
        def sb(name, shape):
            return ctx.enter_context(nc.sbuf_tensor(name, shape, F32))

        def mark(name, step=1):
            return Mark(nc, ctx, name, step)

        w_in_sb = sb("w_in_sb", [P, DC, 2 * ED])
        wx_sb = sb("wx_sb", [P, 2, EC, NP])
        wdt_sb = sb("wdt_sb", [DTR, 2, ED])
        w_out_sb = sb("w_out_sb", [P, EC, D])
        chan_sb = sb("chan_sb", [P, EC, 2 * NCH])
        neg_a = sb("neg_a", [P, EC, 2, N])
        ident = sb("ident", [P, P])
        router_sb = sb("router_sb", [P, DC, E])
        router_b_sb = sb("router_b_sb", [P, E])
        b1_sb = sb("b1_sb", [P, HC, NX])
        b2_sb = sb("b2_sb", [NX, D])
        rank = sb("rank", [P, TB, E])
        minus_half = sb("minus_half", [P, TB])
        expert_w = sb("expert_w", [P, 3, DC * H])

        xu = sb("xu", [P, 2, EC, L])
        delta = sb("delta", [P, EC, L])
        sp_tmp = sb("sp_tmp", [P, L])
        h = sb("h", [P, 2, EC, L])
        b_row = sb("b_row", [P, N_B_ROW, L])
        drive = sb("drive", [P, N_DRIVE, L])
        y = sb("y", [P, TB, ED])
        xn_t = sb("xn_t", [P, DC, L])
        dbc = sb("dbc", [NP, L])
        c_col = sb("c_col", [P, 2, TB, N])
        xn2_t = sb("xn2_t", [P, DC, L])
        acc = sb("acc", [P, TB, D])
        work = sb("work", [P, 2 * HC * BANK + L])
        prep_work = sb("prep_work", [P, L + XZW])
        norm_scratch = [(sb(f"stats{i}", [P, TB, 6]), sb(f"mv{i}", [P, TB, 2]), sb(f"rstd{i}", [P, TB]))
                        for i in range(2)]
        logits = sb("logits", [P, TB, E])
        sel1 = sb("sel1", [P, TB, E])
        sel2 = sb("sel2", [P, TB, E])
        cand = sb("cand", [P, TB, E])
        peak = sb("peak", [P, TB])
        mix = sb("mix", [P, TB, NX])

        half = HC * BANK
        prep_half = prep_work[:, 0:L]
        prep_tokens = prep_half.rearrange("p (b d) -> p b d", d=D)
        xz_pad = prep_work[:, L:L + XZW]
        tokens = work[:, 0:TB * D].rearrange("p (b d) -> p b d", b=TB)
        z_half = work[:, 0:half].rearrange("p (c t) -> p c t", c=EC)
        y_half = work[:, half:2 * half].rearrange("p (q e) -> p q e", q=QB)
        dx_half = work[:, 2 * half:2 * half + 2 * BANK].rearrange("p (k t) -> p k t", k=2)
        h1 = work[:, 0:2 * half].rearrange("p (g m t) -> p g m t", g=2, m=HC)
        mix_t = work[0:NX, 2 * half:2 * half + L]

        decay = sb("decay", [P, N_DECAY, L])
        h_t = [ctx.enter_context(nc.psum_tensor(f"h_t{i}", [P, ED], F32)) for i in range(N_H_T)]
        side = [ctx.enter_context(nc.psum_tensor(f"side{i}", [P, BANK], F32)) for i in range(N_SIDE)]

        b_dram = nc.dram_tensor("b_dram", [2, N, L], F32, kind="Internal").ap()
        xn_dram = nc.dram_tensor("xn_dram", [2, P, DC * L], F32, kind="Internal").ap()
        xz_dram = nc.dram_tensor("xz_dram", [EC, P, L], F32, kind="Internal").ap()
        dx_dram = nc.dram_tensor("dx_dram", [2, 2, EC, P, L], F32, kind="Internal").ap()
        y_dram = nc.dram_tensor("y_dram", [L, ED], F32, kind="Internal").ap()
        x1_dram = nc.dram_tensor("x1_dram", [P, TB * D], F32, kind="Internal").ap()

        pe, dve, act, pool, sp = (Lane(e) for e in (nc.tensor, nc.vector, nc.scalar, nc.gpsimd, nc.sync))

        m_const = mark("m_const", 16)
        m_ident = mark("m_ident")
        m_neg_a = mark("m_neg_a")
        m_setup_pool = mark("m_setup_pool")
        m_decay = mark("m_decay")
        m_drive = mark("m_drive")
        m_scan = mark("m_scan")
        m_turn = mark("m_turn")
        m_y = mark("m_y")
        m_dt_mm = mark("m_dt_mm")
        m_dt_act = mark("m_dt_act")
        m_delta = mark("m_delta")
        m_u = mark("m_u")
        m_brow = [mark(f"m_brow{i}", 16) for i in range(N_B_ROW)]
        m_bdram = mark("m_bdram", 16)
        m_ydump = [mark(f"m_ydump{i}", 16) for i in range(TB)]
        m_side_mm = mark("m_side_mm")
        m_side_act = mark("m_side_act")
        m_side_dve = mark("m_side_dve")
        m_side_pool = mark("m_side_pool")
        m_tok = mark("m_tok", 16)
        m_xnst = mark("m_xnst", 16)
        m_xnld = mark("m_xnld", 16)
        m_dxst = mark("m_dxst", 16)
        m_ptok = mark("m_ptok", 16)
        m_dxld = [mark(f"m_dxld{k}", 16) for k in range(2)]
        m_yld = mark("m_yld", 16)
        m_xzst = mark("m_xzst", 16)
        m_xzld = mark("m_xzld", 16)
        m_x1st = mark("m_x1st", 16)
        m_x1ld = mark("m_x1ld", 16)
        m_ew = [mark(f"m_ew{i}", 16) for i in range(3)]
        m_out = mark("m_out", 16)

        loads = [
            (w_in_sb[:, :, :], w_in_t.rearrange("(c p) e -> p c e", p=P)),
            (chan_sb[:, :, :], chan.rearrange("(c p) k -> p c k", p=P)),
            (wx_sb[:, 0, :, :], wx_t[0].rearrange("(c p) k -> p c k", p=P)),
            (wx_sb[:, 1, :, :], wx_t[1].rearrange("(c p) k -> p c k", p=P)),
            (wdt_sb[:, 0, :], wdt_t[0]),
            (wdt_sb[:, 1, :], wdt_t[1]),
            (w_out_sb[:, :, :], w_out_t.rearrange("(c p) d -> p c d", p=P)),
            (router_sb[:, :, :], router_w.rearrange("(c p) e -> p c e", p=P)),
            (router_b_sb[:, :], router_b.rearrange("(a e) -> a e", a=1).to_broadcast([P, E])),
            (b1_sb[:, :, :], b1_t.rearrange("(m p) x -> p m x", p=P)),
            (b2_sb[:, :], b2),
        ]
        for dst, src in loads:
            consts = m_const.on(sp.e.dma_start(dst, src))

        pool.need(m_ident.on(pool.e.memset(ident[:, :], 0.0)))
        ident_ready = m_ident.on(pool.e.affine_select(
            out=ident[:, :], in_=ident[:, :], compare_op=ALU.not_equal, fill=1.0, base=0,
            pattern=[[-1, P]], channel_multiplier=1))
        minus_half_ready = m_setup_pool.on(pool.e.memset(minus_half[:, :], -0.5))
        for e in range(E):
            rank_ready = m_setup_pool.on(pool.e.memset(rank[:, :, e:e + 1], float(E - e)))
        ones_ready = m_setup_pool.on(pool.e.memset(mix[:, :, E:NX], 1.0))

        act.e.preload_act_table_set("natural_log_exp_and_others")
        act.need(consts)
        for d in range(2):
            k = d * NCH + CHAN_A
            ea = m_neg_a.on(act.e.activation(neg_a[:, :, d, :], chan_sb[:, :, k:k + N], ACT.Exp))
        act.need(ea)
        neg_a_ready = m_neg_a.on(act.e.mul(neg_a[:, :, :, :], neg_a[:, :, :, :], -1.0))

        def chan_col(d, c, k):
            return chan_sb[:, c, d * NCH + k:d * NCH + k + 1]

        bank_free = [None] * N_SIDE
        bank_held = [False] * N_SIDE
        bank_next = [0]

        def take_bank():
            i = next(j % N_SIDE for j in range(bank_next[0], bank_next[0] + N_SIDE) if not bank_held[j % N_SIDE])
            bank_next[0] = (i + 1) % N_SIDE
            bank_held[i] = True
            pe.need(bank_free[i])
            return i

        def give_bank(i, token):
            bank_free[i] = token
            bank_held[i] = False

        def products(dst, pairs, m):
            for i, (lhs, rhs) in enumerate(pairs):
                last = pe.e.matmul(dst, lhs, rhs, start=(i == 0), stop=(i == len(pairs) - 1))
            return m.on(last)

        def turns(items, m):
            for dst, src in items:
                k = src.shape[0]
                last = pe.e.transpose(dst, src, ident[0:k, 0:k])
            return m.on(last)

        decay_done, drive_done, scan_done = {}, {}, {}
        turn_done, y_done = {}, {}
        delta_ready, u_ready, x_ready, x_read = {}, {}, {}, {}
        dbc_ready, dbc_read, c_ready, b_stored, b_row_ready = {}, {}, {}, {}, {}
        y_dumped, y_loaded = {}, {}
        xz_stored, xz_loaded = {}, {}
        xn_ready, xn_stored, xn_loaded = {}, {}, {}
        dx_stored, dx_loaded = {}, {}
        xn_t_read = [None]
        work_read = []
        prep_read = []
        acc_read = [None]
        xn2_read = [None]
        x1_loaded = [None]
        x1_stored = [None]
        mix_read = [None]

        def hand_over(*marks):
            work_read[:] = [m for m in marks if m is not None]

        def start_chunk(w, c):
            b, d = divmod(w, 2)
            banks = []
            for s in range(NH):
                i = take_bank()
                pe.need(dbc_ready[w])
                mm = products(side[i][:, :], [(wdt_sb[:, d, c * P:(c + 1) * P],
                                               dbc[0:DTR, s * BANK:(s + 1) * BANK])], m_dt_mm)
                banks.append((i, mm))
            dbc_read[w] = mm
            yield
            for s, (i, mm) in enumerate(banks):
                act.need(mm, decay_done.get(w * UNITS - EC + c))
                pre = m_dt_act.on(act.e.activation(delta[:, c, s * BANK:(s + 1) * BANK], side[i][:, :],
                                                   ACT.Identity, bias=chan_col(d, c, CHAN_B_DT)))
                give_bank(i, pre)
            yield
            act.need(pre, delta_ready.get("last"))
            tmp = m_dt_act.on(act.e.activation(sp_tmp[:, :], delta[:, c, :], ACT.Abs))
            act.need(tmp)
            tmp = m_dt_act.on(act.e.activation(sp_tmp[:, :], sp_tmp[:, :], ACT.Exp, scale=-1.0))
            act.need(tmp)
            tmp = m_dt_act.on(act.e.activation(sp_tmp[:, :], sp_tmp[:, :], ACT.Ln, bias=1.0))
            yield
            dve.need(tmp)
            delta_ready[w, c] = delta_ready["last"] = m_delta.on(dve.e.scalar_tensor_tensor(
                out=delta[:, c, :], in0=delta[:, c, :], scalar=0.0, in1=sp_tmp[:, :],
                op0=ALU.max, op1=ALU.add))
            pool.need(delta_ready[w, c], x_ready[w], x_read[w])
            u_ready[w, c] = m_u.on(pool.e.tensor_tensor(xu[:, d, c, :], xu[:, d, c, :], delta[:, c, :], ALU.mult))

        def load_b_row(gn):
            w, n = divmod(gn, N)
            sp.need(b_stored[w], drive_done.get((gn - N_B_ROW) * EC + EC - 1))
            b_row_ready[gn] = m_brow[gn % N_B_ROW].on(sp.e.dma_start(
                b_row[:, gn % N_B_ROW, :], b_dram[w % 2, n:n + 1, :].to_broadcast([P, L])))

        def feed_unit(k):
            gn, c = divmod(k, EC)
            w, n = divmod(gn, N)
            d = w % 2
            act.need(neg_a_ready, delta_ready[w, c], scan_done.get(k - N_DECAY))
            decay_done[k] = m_decay.on(act.e.activation(decay[:, k % N_DECAY, :], delta[:, c, :], ACT.Exp,
                                                        scale=neg_a[:, c, d, n:n + 1]))
            pool.need(u_ready[w, c], b_row_ready[gn], scan_done.get(k - N_DRIVE))
            drive_done[k] = m_drive.on(pool.e.tensor_tensor(drive[:, k % N_DRIVE, :], xu[:, d, c, :],
                                                            b_row[:, gn % N_B_ROW, :], ALU.mult))

        def scan_unit(k):
            gn, c = divmod(k, EC)
            d = (gn // N) % 2
            dve.need(decay_done[k], drive_done[k], turn_done.get((gn - 2) * TB + TB - 1))
            o, a, v = h[:, gn % 2, c, :], decay[:, k % N_DECAY, :], drive[:, k % N_DRIVE, :]
            if d:
                o, a, v = h[:, gn % 2, c, ::-1], decay[:, k % N_DECAY, ::-1], drive[:, k % N_DRIVE, ::-1]
            scan_done[k] = m_scan.on(dve.e.tensor_tensor_scan(o, a, v, 0.0, ALU.mult, ALU.add))

        def turn_tile(i):
            gn, tb = divmod(i, TB)
            pe.need(ident_ready, scan_done[gn * EC + EC - 1], y_done.get(i - N_H_T))
            turn_done[i] = turns([(h_t[i % N_H_T][:, c * P:(c + 1) * P],
                                   h[:, gn % 2, c, tb * P:(tb + 1) * P]) for c in range(EC)], m_turn)

        def sum_tile(i):
            gn, tb = divmod(i, TB)
            w, n = divmod(gn, N)
            b, d = divmod(w, 2)
            c_n = c_col[:, w % 2, tb, n:n + 1]
            if d == 0 and n == 0:
                dve.need(turn_done[i], c_ready[w], y_dumped.get((b - 1, tb)))
                y_done[i] = m_y.on(dve.e.tensor_scalar(y[:, tb, :], h_t[i % N_H_T][:, :], c_n, None, ALU.mult))
            else:
                dve.need(turn_done[i], c_ready[w], y_done[i - TB])
                y_done[i] = m_y.on(dve.e.scalar_tensor_tensor(
                    out=y[:, tb, :], in0=h_t[i % N_H_T][:, :], scalar=c_n, in1=y[:, tb, :],
                    op0=ALU.mult, op1=ALU.add))
            if d == 1 and n == N - 1:
                sp.need(y_done[i], y_loaded.get((b - 1, tb)))
                y_dumped[b, tb] = m_ydump[tb].on(sp.e.dma_start(y_dram[tb * P:(tb + 1) * P, :], y[:, tb, :]))

        def paced(jobs):
            waiting = []
            for job in jobs:
                if job is not None:
                    produce, read, cost = job
                    waiting.append((read, produce() if produce else ()))
                    yield cost
                while len(waiting) > (PACE if job else 0):
                    read, args = waiting.pop(0)
                    read(*args)
                    if job is None:
                        yield 0.3
                if job is None:
                    yield LATENCY
                    yield LATENCY
            for read, args in waiting:
                read(*args)
                yield 0.3
            yield LATENCY

        def norm_tokens(src, dst, token, scratch):
            stats, mv, rstd = norm_scratch[scratch]
            n = src.shape[1]
            dve.need(token)
            for tb in range(n):
                st = m_side_dve.on(dve.e.bn_stats(stats[:, tb, :], src[:, tb, :]))
            yield LATENCY
            dve.need(st)
            for tb in range(n):
                st = m_side_dve.on(dve.e.bn_aggr(mv[:, tb, :], stats[:, tb, :]))
            dve.need(st)
            st = m_side_dve.on(dve.e.tensor_scalar(rstd[:, 0:n], mv[:, 0:n, 1], EPS, None, ALU.add))
            pool.need(st, minus_half_ready)
            r = m_side_pool.on(pool.e.tensor_tensor(rstd[:, 0:n], rstd[:, 0:n], minus_half[:, 0:n], ALU.pow))
            yield LATENCY
            yield LATENCY
            dve.need(r)
            for tb in range(n):
                st = m_side_dve.on(dve.e.tensor_scalar(dst[:, tb, :], src[:, tb, :], mv[:, tb, 0:1],
                                                       rstd[:, tb:tb + 1], ALU.subtract, ALU.mult))
                if tb == n // 2:
                    yield LATENCY
            return st

        def turn_tokens(src, dst, at, token, dst_free):
            last = {}

            def jobs():
                for c in range(DC):
                    for s in range(src.shape[1] // QB):
                        def produce(c=c, s=s):
                            i = take_bank()
                            pe.need(token, ident_ready)
                            last["turned"] = turns([
                                (side[i][:, q * P:(q + 1) * P], src[:, s * QB + q, c * P:(c + 1) * P])
                                for q in range(QB)], m_side_mm)
                            return i, last["turned"]

                        def read(i, t, c=c, s=s):
                            act.need(t, dst_free)
                            last["copied"] = m_side_act.on(act.e.copy(
                                dst[:, c, at + s * BANK:at + (s + 1) * BANK], side[i][:, :]))
                            give_bank(i, last["copied"])

                        yield produce, read, 0.5

            yield from paced(jobs())
            return last["turned"], last["copied"]

        def prepare(w):
            b, d = divmod(w, 2)
            busy = tuple(prep_read)
            tokens_turned = None
            if d == 0:
                for s in range(NH):
                    sp.need(tokens_turned, *busy)
                    t = m_ptok.on(sp.e.dma_start(prep_tokens[:, :, :], x[b, s * BANK:(s + 1) * BANK, :].rearrange(
                        "(b p) d -> p b d", p=P)))
                    yield LATENCY
                    normed = yield from norm_tokens(prep_tokens, prep_tokens, t, 0)
                    tokens_turned, xn_ready[b] = yield from turn_tokens(prep_tokens, xn_t, s * BANK, normed, xn_t_read[0])
                sp.need(xn_ready[b], xn_loaded.get(b - 2))
                xn_stored[b] = m_xnst.on(sp.e.dma_start(xn_dram[b % 2], xn_t[:, :, :].rearrange("p c t -> p (c t)")))
            pool.need(*busy)
            pool.e.memset(xz_pad[:, 0:PAD], 0.0)
            pads = m_side_pool.on(pool.e.memset(xz_pad[:, PAD + L:XZW], 0.0))
            buffer_free = drive_done.get((w - 1) * UNITS - 1)
            starts = [PAD + (TAPS - 1 - k) * (1 if d else -1) for k in range(TAPS)]
            got = {}
            pe.need(consts)

            def load_xz(c):
                sp.need(xz_stored[b, c], got.get("tap"), pads, *busy)
                got[c] = xz_loaded[b, c] = m_xzld.on(sp.e.dma_start(xz_pad[:, PAD:PAD + L], xz_dram[c]))

            def project_jobs():
                for c in range(EC):
                    if d == 1:
                        yield None, (lambda c=c: load_xz(c)), LATENCY
                        yield None, (lambda: None), LATENCY
                    else:
                        for s in range(NH):
                            def produce(c=c, s=s):
                                i = take_bank()
                                pe.need(xn_ready[b])
                                return i, products(side[i][:, :], [
                                    (w_in_sb[:, k, c * P:(c + 1) * P], xn_t[:, k, s * BANK:(s + 1) * BANK])
                                    for k in range(DC)], m_side_mm)

                            def read(i, mm, c=c, s=s):
                                act.need(mm, got.get("tap"), xz_stored.get((b, c - 1)), *busy)
                                got[c] = m_side_act.on(act.e.copy(
                                    xz_pad[:, PAD + s * BANK:PAD + (s + 1) * BANK], side[i][:, :]))
                                give_bank(i, got[c])
                                if s == NH - 1:
                                    sp.need(got[c], xz_loaded.get((b - 1, c)))
                                    xz_stored[b, c] = m_xzst.on(sp.e.dma_start(xz_dram[c], xz_pad[:, PAD:PAD + L]))

                            yield produce, read, 1.8
                    for k in range(TAPS):
                        def tap(c=c, k=k):
                            zb = xz_pad[:, starts[k]:starts[k] + L]
                            dve.need(got[c], pads, buffer_free, got.get("tap"))
                            if k == 0:
                                op = dve.e.tensor_scalar(xu[:, d, c, :], zb, chan_col(d, c, CHAN_CONV_W),
                                                         chan_col(d, c, CHAN_CONV_B), ALU.mult, ALU.add)
                            else:
                                op = dve.e.scalar_tensor_tensor(
                                    out=xu[:, d, c, :], in0=zb, scalar=chan_col(d, c, CHAN_CONV_W + k),
                                    in1=xu[:, d, c, :], op0=ALU.mult, op1=ALU.add)
                            got["tap"] = m_side_dve.on(op)

                        yield None, tap, TAP_COST

            yield from paced(project_jobs())
            act.need(got["tap"])
            x_ready[w] = m_side_act.on(act.e.activation(xu[:, d, :, :], xu[:, d, :, :], ACT.Silu))
            act.e.preload_act_table_set("natural_log_exp_and_others")
            yield LATENCY
            yield LATENCY
            yield LATENCY

            def later_jobs():
                for s in range(NH):
                    def produce(s=s):
                        i = take_bank()
                        pe.need(x_ready[w])
                        x_read[w] = products(side[i][0:NP, :], [
                            (wx_sb[:, d, c, :], xu[:, d, c, s * BANK:(s + 1) * BANK]) for c in range(EC)], m_side_mm)
                        return i, x_read[w]

                    def read(i, mm, s=s):
                        act.need(mm, dbc_read.get(w - 1), b_stored.get(w - 1), c_ready.get(w - 1))
                        dbc_ready[w] = m_side_act.on(act.e.copy(dbc[:, s * BANK:(s + 1) * BANK], side[i][0:NP, :]))
                        give_bank(i, dbc_ready[w])

                    yield produce, read, 3.6
                for c in range(EC):
                    def scale_by_d(c=c):
                        act.need(x_ready[w], tokens_turned, dx_stored.get((w, c - 1)), *busy)
                        e = m_side_act.on(act.e.mul(prep_half, xu[:, d, c, :], chan_col(d, c, CHAN_D)))
                        sp.need(e, dx_loaded.get((b - 2, d)))
                        dx_stored[w, c] = m_dxst.on(sp.e.dma_start(dx_dram[b % 2, d, c], prep_half))

                    yield None, scale_by_d, LATENCY
                    yield None, (lambda: None), LATENCY
                yield None
                sp.need(dbc_ready[w], *(b_row_ready.get((w - 1) * N - 1 - i) for i in range(N_B_ROW)))
                b_stored[w] = m_bdram.on(sp.e.dma_start(b_dram[w % 2], dbc[DTR:DTR + N, :]))
                for s in range(NH):
                    def produce(s=s):
                        i = take_bank()
                        pe.need(dbc_ready[w])
                        return i, turns([(side[i][:, q * NP:(q + 1) * NP],
                                          dbc[:, (s * QB + q) * P:(s * QB + q + 1) * P]) for q in range(QB)], m_side_mm)

                    def read(i, t, s=s):
                        act.need(t, y_done.get((w - 1) * N * TB - 1))
                        c_ready[w] = m_side_act.on(act.e.copy(
                            c_col[:, w % 2, s * QB:(s + 1) * QB, :],
                            side[i][:, 0:QB * NP].rearrange("p (q k) -> p q k", q=QB)[:, :, DTR + N:NP]))
                        give_bank(i, c_ready[w])

                    yield produce, read, 0.5

            yield from paced(later_jobs())
            prep_read[:] = [got["tap"], dx_stored[w, EC - 1], xz_stored[b, EC - 1]]

        def gate(b):
            busy = tuple(work_read)
            sp.need(xn_t_read[0], xn_stored[b])
            xn_loaded[b] = m_xnld.on(sp.e.dma_start(xn_t[:, :, :].rearrange("p c t -> p (c t)"), xn_dram[b % 2]))
            got = {}

            def load_y(s):
                rows = y_dram[s * BANK:(s + 1) * BANK, :].rearrange("(q p) e -> p q e", p=P)
                sp.need(*(y_dumped[b, s * QB + q] for q in range(QB)), got.get("y turned"), *busy)
                got["y", s] = m_yld.on(sp.e.dma_start(y_half[:, :, :], rows))
                for q in range(QB):
                    y_loaded[b, s * QB + q] = got["y", s]

            def load_dx(j):
                s, c = divmod(j, EC)
                for k in range(2):
                    sp.need(dx_stored[2 * b + k, c], got.get("gated"), *busy)
                    got["dx", j, k] = dx_loaded[b, k] = m_dxld[k].on(sp.e.dma_start(
                        dx_half[:, k, :], dx_dram[b % 2, k, c, :, s * BANK:(s + 1) * BANK]))

            def jobs():
                load_y(0)
                load_dx(0)
                for s in range(NH):
                    for c in range(EC):
                        def produce(s=s, c=c):
                            i = take_bank()
                            pe.need(xn_loaded[b])
                            got["z mm"] = products(side[i][:, :], [
                                (w_in_sb[:, k, ED + c * P:ED + (c + 1) * P], xn_t[:, k, s * BANK:(s + 1) * BANK])
                                for k in range(DC)], m_side_mm)
                            return i, got["z mm"]

                        def read(i, mm, c=c):
                            act.need(mm, got.get("projected"), *busy)
                            got["z"] = m_side_act.on(act.e.copy(z_half[:, c, :], side[i][:, :]))
                            give_bank(i, got["z"])
                            if c == EC - 1:
                                act.need(got["z"])
                                got["z"] = m_side_act.on(act.e.activation(z_half[:, :, :], z_half[:, :, :], ACT.Silu))
                                act.e.preload_act_table_set("natural_log_exp_and_others")

                        yield produce, read, 1.8
                    for c in range(EC):
                        def produce(s=s, c=c):
                            i = take_bank()
                            pe.need(got["y", s])
                            got["y turned"] = turns([(side[i][:, q * P:(q + 1) * P], y_half[:, q, c * P:(c + 1) * P])
                                                     for q in range(QB)], m_side_mm)
                            return i, got["y turned"]

                        def add(i, t, s=s, c=c):
                            j = s * EC + c
                            a = dx_half[:, 0, :]
                            dve.need(t, got["dx", j, 0])
                            v = m_side_dve.on(dve.e.tensor_tensor(a, side[i][:, :], a, ALU.add))
                            give_bank(i, v)
                            pool.need(v, got["dx", j, 1])
                            v = m_side_pool.on(pool.e.tensor_tensor(a, a, dx_half[:, 1, :], ALU.add))
                            pool.need(v, got["z"])
                            got["gated"] = m_side_pool.on(pool.e.tensor_tensor(
                                z_half[:, c, :], z_half[:, c, :], a, ALU.mult))
                            if j + 1 < NH * EC:
                                load_dx(j + 1)

                        yield produce, add, 0.8
                        yield None, (lambda: None), LATENCY
                    yield None
                    if s + 1 < NH:
                        load_y(s + 1)
                    for q in range(QB):
                        def produce(q=q):
                            i = take_bank()
                            pe.need(got["gated"])
                            got["projected"] = products(side[i][:, 0:D], [
                                (z_half[:, c, q * P:(q + 1) * P], w_out_sb[:, c, :]) for c in range(EC)], m_side_mm)
                            return i, got["projected"]

                        def read(i, mm, tb=s * QB + q):
                            act.need(mm, acc_read[0])
                            got["o"] = m_side_act.on(act.e.mul(acc[:, tb, :], side[i][:, 0:D], 0.5))
                            give_bank(i, got["o"])

                        yield produce, read, 1.8

            yield from paced(jobs())
            xn_t_read[0] = got["z mm"]
            sp.need(got["projected"])
            t = m_tok.on(sp.e.dma_start(tokens[:, :, :], x[b].rearrange("(b p) d -> p b d", p=P)))
            normed = yield from norm_tokens(acc, acc, got["o"], 1)
            dve.need(normed, t)
            r = m_side_dve.on(dve.e.tensor_tensor(acc[:, :, :], acc[:, :, :], tokens[:, :, :], ALU.add))
            sp.need(r, x1_loaded[0])
            x1_stored[0] = m_x1st.on(sp.e.dma_start(x1_dram, acc[:, :, :].rearrange("p b d -> p (b d)")))
            yield LATENCY
            normed = yield from norm_tokens(acc, tokens, r, 1)
            tokens_turned, xn2_ready[0] = yield from turn_tokens(tokens, xn2_t, 0, normed, xn2_read[0])
            hand_over(tokens_turned)

        xn2_ready = [None]

        def route(b):
            busy = tuple(work_read)
            i = take_bank()
            pe.need(xn2_ready[0])
            for tb in range(TB):
                lg = products(side[i][:, tb * E:(tb + 1) * E],
                              [(xn2_t[:, k, tb * P:(tb + 1) * P], router_sb[:, k, :]) for k in range(DC)], m_side_mm)
            yield 1.5
            dve.need(lg)
            v = m_side_dve.on(dve.e.tensor_tensor(
                logits[:, :, :], side[i][:, 0:TB * E].rearrange("p (b e) -> p b e", b=TB),
                router_b_sb[:, :].rearrange("p (a e) -> p a e", a=1).to_broadcast([P, TB, E]), ALU.add))
            give_bank(i, v)

            def step(instruction):
                v = m_side_dve.on(instruction)
                dve.need(v)
                return v

            def wide():
                return peak[:, :].rearrange("p (b a) -> p b a", a=1).to_broadcast([P, TB, E])

            dve.need(v)
            step(dve.e.tensor_reduce(peak[:, :], logits[:, :, :], AX_X, ALU.max))
            v = step(dve.e.tensor_tensor(logits[:, :, :], logits[:, :, :], wide(), ALU.subtract))
            act.need(v)
            v = m_side_act.on(act.e.activation(logits[:, :, :], logits[:, :, :], ACT.Exp))
            yield LATENCY
            yield LATENCY
            dve.need(v)
            step(dve.e.tensor_reduce(peak[:, :], logits[:, :, :], AX_X, ALU.add))
            step(dve.e.reciprocal(peak[:, :], peak[:, :]))
            step(dve.e.tensor_tensor(logits[:, :, :], logits[:, :, :], wide(), ALU.mult))
            dve.need(rank_ready, ones_ready, mix_read[0])

            def first_of_largest(p, sel):
                step(dve.e.tensor_reduce(peak[:, :], p, AX_X, ALU.max))
                step(dve.e.tensor_tensor(cand[:, :, :], p, wide(), ALU.is_equal))
                step(dve.e.tensor_tensor(cand[:, :, :], cand[:, :, :], rank[:, :, :], ALU.mult))
                step(dve.e.tensor_reduce(peak[:, :], cand[:, :, :], AX_X, ALU.max))
                step(dve.e.tensor_tensor(sel, cand[:, :, :], wide(), ALU.is_equal))

            first_of_largest(logits[:, :, :], sel1[:, :, :])
            yield LATENCY
            step(dve.e.scalar_tensor_tensor(out=mix[:, :, 0:E], in0=sel1[:, :, :], scalar=-2.0,
                                            in1=logits[:, :, :], op0=ALU.mult, op1=ALU.add))
            first_of_largest(mix[:, :, 0:E], sel2[:, :, :])
            step(dve.e.tensor_tensor(sel1[:, :, :], sel1[:, :, :], sel2[:, :, :], ALU.add))
            mixed = step(dve.e.tensor_tensor(mix[:, :, 0:E], logits[:, :, :], sel1[:, :, :], ALU.mult))
            yield LATENCY

            def jobs():
                for s in range(NH):
                    def produce(s=s):
                        i = take_bank()
                        pe.need(mixed)
                        return i, turns([(side[i][0:NX, q * P:(q + 1) * P], mix[:, s * QB + q, :])
                                         for q in range(QB)], m_side_mm)

                    def read(i, t, s=s):
                        act.need(t, *busy)
                        got["mix_t"] = m_side_act.on(act.e.copy(mix_t[:, s * BANK:(s + 1) * BANK], side[i][0:NX, :]))
                        give_bank(i, got["mix_t"])

                    yield produce, read, 0.5
                yield None
                for tb in range(TB):
                    def produce(tb=tb):
                        i = take_bank()
                        pe.need(got["mix_t"])
                        got["bias mm"] = products(side[i][:, 0:D], [(mix_t[:, tb * P:(tb + 1) * P], b2_sb[:, :])],
                                                  m_side_mm)
                        return i, got["bias mm"]

                    def read(i, mm, tb=tb):
                        act.need(mm, x1_stored[0])
                        acc_done[tb] = m_side_act.on(act.e.copy(acc[:, tb, :], side[i][:, 0:D]))
                        give_bank(i, acc_done[tb])

                    yield produce, read, 0.6

            got = {}
            yield from paced(jobs())
            hand_over(*busy, got["bias mm"])

        acc_done = {}
        expert_loaded, expert_read = {}, {}

        def load_expert(s):
            if s >= 2 * NX * NB or s in expert_loaded:
                return
            xp, k = divmod(s % (2 * NX), 2)
            src = w1[xp].rearrange("(c p) n -> p c n", p=P) if k == 0 else w2[xp].rearrange("(c p) n -> p c n", p=P)
            sp.need(expert_read.get(s - 3))
            expert_loaded[s] = m_ew[s % 3].on(sp.e.dma_start(
                expert_w[:, s % 3, :].rearrange("p (c n) -> p c n", n=src.shape[2]), src))

        h1_read = [None, None]

        def experts(b, first, last):
            busy = tuple(work_read)
            hid = {}
            last_read = {}

            def jobs():
                for xp in range(first, last):
                    s = 2 * (b * NX + xp)
                    load_expert(s)
                    load_expert(s + 1)
                    wi = expert_w[:, s % 3, :].rearrange("p (c n) -> p c n", n=H)
                    wo = expert_w[:, (s + 1) % 3, :].rearrange("p (c n) -> p c n", n=D)
                    for g in range(NH):
                        for m in range(HC):
                            def produce(s=s, wi=wi, g=g, m=m):
                                i = take_bank()
                                pe.need(expert_loaded[s], xn2_ready[0])
                                mm = products(side[i][:, :], [(wi[:, k, m * P:(m + 1) * P],
                                                               xn2_t[:, k, g * BANK:(g + 1) * BANK])
                                                              for k in range(DC)], m_side_mm)
                                if g == NH - 1 and m == HC - 1:
                                    expert_read[s] = mm
                                    load_expert(s + 2)
                                return i, mm

                            def read(i, mm, xp=xp, g=g, m=m):
                                act.need(mm, h1_read[g], *busy)
                                e = m_side_act.on(act.e.activation(h1[:, g, m, :], side[i][:, :], ACT.Identity,
                                                                   bias=b1_sb[:, m, xp:xp + 1]))
                                give_bank(i, e)
                                if m == HC - 1:
                                    act.need(e)
                                    hid[g] = m_side_act.on(act.e.activation(h1[:, g, :, :], h1[:, g, :, :], ACT.Gelu))
                                    act.e.preload_act_table_set("natural_log_exp_and_others")

                            yield produce, read, 1.8
                    for g in range(NH):
                        for q in range(QB):
                            def produce(s=s, wo=wo, g=g, q=q):
                                i = take_bank()
                                pe.need(hid[g], expert_loaded[s + 1])
                                mm = products(side[i][:, 0:D], [(h1[:, g, m, q * P:(q + 1) * P], wo[:, m, :])
                                                                for m in range(HC)], m_side_mm)
                                if q == QB - 1:
                                    h1_read[g] = expert_read[s + 1] = mm
                                last_read[0] = mm
                                return i, mm

                            def read(i, mm, xp=xp, tb=g * QB + q):
                                dve.need(mm, acc_done[tb])
                                acc_done[tb] = m_side_dve.on(dve.e.scalar_tensor_tensor(
                                    out=acc[:, tb, :], in0=side[i][:, 0:D], scalar=mix[:, tb, xp:xp + 1],
                                    in1=acc[:, tb, :], op0=ALU.mult, op1=ALU.add))
                                give_bank(i, acc_done[tb])

                            yield produce, read, 1.8

            yield from paced(jobs())
            hand_over(*busy, last_read[0])
            if last == NX:
                xn2_read[0] = last_read[0]
                mix_read[0] = acc_done[TB - 1]

        def finish(b):
            busy = tuple(work_read)
            sp.need(x1_stored[0], *busy)
            x1_loaded[0] = m_x1ld.on(sp.e.dma_start(tokens[:, :, :].rearrange("p b d -> p (b d)"), x1_dram))
            normed = yield from norm_tokens(acc, acc, acc_done[TB - 1], 1)
            dve.need(normed, x1_loaded[0])
            r = m_side_dve.on(dve.e.tensor_tensor(acc[:, :, :], acc[:, :, :], tokens[:, :, :], ALU.add))
            sp.need(r)
            acc_read[0] = m_out.on(sp.e.dma_start(out[b].rearrange("(b p) d -> p b d", p=P), acc[:, :, :]))
            hand_over(r)

        def expert_stream(b):
            yield from gate(b)
            yield from route(b)
            yield from experts(b, 0, NX)
            yield from finish(b)

        for _ in prepare(0):
            pass
        NU = NW * UNITS

        starting = {}

        def start_stages(k):
            for stage, lead in ((3, 1), (2, EC - 2), (1, EC - 1), (0, EC)):
                w, c = divmod(k + lead, UNITS)
                if c < EC and w < NW and w > 0:
                    if stage == 0:
                        starting[w, c] = start_chunk(w, c)
                    next(starting[w, c], None)

        def feed(k):
            start_stages(k)
            if k % EC == 0 and k + 2 * EC < NU:
                load_b_row(k // EC + 2)
            if k < NU:
                feed_unit(k)

        for c in range(EC):
            for _ in start_chunk(0, c):
                pass
        load_b_row(0)
        load_b_row(1)
        for k in range(LOOKAHEAD):
            feed(k)
        tiles_turned = 0
        for k in range(NU + EC):
            w, unit = divmod(k, UNITS)
            if w < NW:
                if unit == 0:
                    preparing = prepare(w + 1) if w + 1 < NW else iter(())
                    prep_due = prep_spent = 0.0
                if unit == EC and w % 2 == 0:
                    mixing = expert_stream(w // 2 - 1) if w else iter(())
                    mix_due = mix_spent = 0.0
                scan_unit(k)
                feed(k + LOOKAHEAD)
            turnable = min(k // EC if (k + 1) % EC else k // EC + 1, NU // EC) * TB
            for half in range(2):
                i = 2 * (k - EC) + half
                while tiles_turned < min(turnable, i + N_H_T):
                    turn_tile(tiles_turned)
                    tiles_turned += 1
                if i >= 0:
                    sum_tile(i)
                if w < NW:
                    prep_due += PREP_COST[w % 2] / (2 * (UNITS - 4 * EC))
                    while prep_spent < prep_due:
                        step = next(preparing, None)
                        if step is None:
                            break
                        prep_spent += step + 0.15
                    if k < EC or (w % 2 == 0 and unit < EC):
                        continue
                    mix_due += MIX_COST / (2 * (2 * UNITS - 4 * EC))
                    while mix_spent < mix_due:
                        step = next(mixing, None)
                        if step is None:
                            break
                        mix_spent += step + 0.15
            if w < NW and unit == UNITS - 3 * EC:
                for _ in preparing:
                    pass
            if w < NW and unit == UNITS - 1 and w % 2:
                for _ in mixing:
                    pass
        for _ in expert_stream(NB - 1):
            pass
        sp.need((m_out, m_out.count), (m_bdram, m_bdram.count), (m_xnst, m_xnst.count), (m_x1st, m_x1st.count),
                (m_dxst, m_dxst.count), (m_xzst, m_xzst.count), *[(m, m.count) for m in m_ydump])


def kernel(**inputs):
    import numpy as np
    import concourse.bacc as bacc
    from concourse.bass_utils import run_bass_kernel_spmd as run

    a = {k: np.asarray(v) for k, v in inputs.items()}

    def chan(s):
        cols = [a["L0_attn_conv_w" + s][:, 0, :], a["L0_attn_conv_b" + s][:, None], a["L0_attn_b_dt" + s][:, None],
                a["L0_attn_Dp" + s][:, None], a["L0_attn_A_log" + s]]
        return np.concatenate(cols, axis=1)

    arrays = {
        "x": a["L0_attn_x"],
        "w_in_t": a["L0_attn_W_in"].T,
        "chan": np.concatenate([chan(""), chan("_b")], axis=1),
        "wx_t": np.stack([a["L0_attn_Wx"].T, a["L0_attn_Wx_b"].T]),
        "wdt_t": np.stack([a["L0_attn_Wdt"].T, a["L0_attn_Wdt_b"].T]),
        "w_out_t": a["L0_attn_W_out"].T,
        "router_w": a["L0_ffn_router_w"],
        "router_b": a["L0_ffn_router_b"],
        "w1": np.concatenate([a["L0_ffn_rw1"], a["L0_ffn_sw1"][None]]),
        "b1_t": np.concatenate([a["L0_ffn_rb1"], a["L0_ffn_sb1"][None]]).T,
        "w2": np.concatenate([a["L0_ffn_rw2"], a["L0_ffn_sw2"][None]]),
        "b2": np.concatenate([a["L0_ffn_rb2"], a["L0_ffn_sb2"][None]]),
    }
    arrays = {f"in_{k}": np.ascontiguousarray(v) for k, v in arrays.items()}
    nc = bacc.Bacc("TRN2", target_bir_lowering=False, num_devices=1,
                    dynamic_dma_scratch_size=DMA_RING_BYTES)
    args = [nc.dram_tensor(k, v.shape, mybir.dt.from_np(v.dtype), kind="ExternalInput").ap() for k, v in arrays.items()]
    out = nc.dram_tensor("out", a["L0_attn_x"].shape, F32, kind="ExternalOutput").ap()
    mamba_moe(nc, *args, out)
    r = run(nc, [arrays], core_ids=[0])
    return r.results[0]["out"]
```

```python
from contextlib import ExitStack

import concourse.bass as bass
from concourse import mybir

F32 = mybir.dt.float32
ALU = mybir.AluOpType
ACT = mybir.ActivationFunctionType
AX_X = mybir.AxisListType.X

P = 128
BANK = 512
TAPS = 4
EPS = 1e-5
DMA_RING_BYTES = 1024
N_DECAY = 3
N_DRIVE = 3
N_B_ROW = 2
N_H_T = 3
N_SIDE = 5
LOOKAHEAD = 2

STEP_COST = 0.2
TAP_COST = 0.6
NORM_COST = 0.5
PAUSE = "pause"
READ_LAG = 1
BARRIER_LAG = 2
MAX_CREDIT = 2.5
PREP_COST = (27.7, 50.0)
PREP_START = (2, 6)
PREP_MARGIN = 32
MIX_COST = 357.3
MIX_MARGIN = 2
CHAN_CONV_W, CHAN_CONV_B, CHAN_B_DT, CHAN_D, CHAN_A = 0, 4, 5, 6, 7


class Mark:

    def __init__(self, nc, ctx, name, step=1):
        self.sem = ctx.enter_context(nc.semaphore(name))
        self.step = step
        self.count = 0

    def on(self, instruction):
        self.count += self.step
        instruction.then_inc(self.sem, self.step)
        return (self, self.count)


class Lane:

    def __init__(self, engine):
        self.e = engine
        self.seen = {}

    def need(self, *marks):
        for m in marks:
            if m is None:
                continue
            mark, count = m
            if self.seen.get(mark, 0) < count:
                self.e.wait_ge(mark.sem, count)
                self.seen[mark] = count


def mamba_moe(nc, x, w_in_t, chan, wx_t, wdt_t, w_out_t, router_w, router_b, w1, b1_t, w2, b2, out):
    NB, L, D = x.shape
    ED = w_out_t.shape[0]
    DTR = wdt_t.shape[1]
    NP = wx_t.shape[2]
    N = (NP - DTR) // 2
    NX = w1.shape[0]
    E = router_w.shape[1]
    H = w1.shape[2]
    NCH = chan.shape[1] // 2
    DC, EC, HC, TB, NH = D // P, ED // P, H // P, L // P, L // BANK
    QB = BANK // P
    assert ED == BANK and H == BANK and L % BANK == 0 and D % P == 0
    PAD = TAPS
    XZW = L + 2 * PAD
    UNITS = N * EC
    NW = 2 * NB
    assert LOOKAHEAD <= min(N_DECAY, N_DRIVE) and PREP_START[0] >= EC - LOOKAHEAD

    ctx = ExitStack()
    with ctx:
        def sb(name, shape):
            return ctx.enter_context(nc.sbuf_tensor(name, shape, F32))

        def mark(name, step=1):
            return Mark(nc, ctx, name, step)

        w_in_sb = sb("w_in_sb", [P, DC, 2 * ED])
        wx_sb = sb("wx_sb", [P, 2, EC, NP])
        wdt_sb = sb("wdt_sb", [DTR, 2, ED])
        w_out_sb = sb("w_out_sb", [P, EC, D])
        chan_sb = sb("chan_sb", [P, EC, 2 * NCH])
        neg_a = sb("neg_a", [P, EC, 2, N])
        ident = sb("ident", [P, P])
        router_sb = sb("router_sb", [P, DC, E])
        router_b_sb = sb("router_b_sb", [P, E])
        b1_sb = sb("b1_sb", [P, HC, NX])
        b2_sb = sb("b2_sb", [NX, D])
        rank = sb("rank", [P, TB, E])
        minus_half = sb("minus_half", [P, TB])
        expert_w = sb("expert_w", [P, 3, DC * H])

        xu = sb("xu", [P, 2, EC, L])
        delta = sb("delta", [P, EC, L])
        h = sb("h", [P, 2, EC, L])
        b_row = sb("b_row", [P, N_B_ROW, L])
        drive = sb("drive", [P, N_DRIVE, L])
        y = sb("y", [P, TB, ED])
        xn_t = sb("xn_t", [P, DC, L])
        dbc = sb("dbc", [NP, L])
        c_col = sb("c_col", [P, 2, TB, N])
        xn2_t = sb("xn2_t", [P, DC, L])
        acc = sb("acc", [P, TB, D])
        work = sb("work", [P, 2 * HC * BANK + L])
        prep_work = sb("prep_work", [P, L + XZW])
        norm_scratch = [(sb(f"stats{i}", [P, TB, 6]), sb(f"mv{i}", [P, TB, 2]), sb(f"rstd{i}", [P, TB]))
                        for i in range(2)]
        logits = sb("logits", [P, TB, E])
        sel1 = sb("sel1", [P, TB, E])
        sel2 = sb("sel2", [P, TB, E])
        cand = sb("cand", [P, TB, E])
        peak = sb("peak", [P, TB])
        mix = sb("mix", [P, TB, NX])

        half = HC * BANK
        prep_half = prep_work[:, 0:L]
        prep_tokens = prep_half.rearrange("p (b d) -> p b d", d=D)
        xz_pad = prep_work[:, L:L + XZW]
        dx_buf = [prep_half, xz_pad[:, PAD:PAD + L]]
        tokens = work[:, 0:TB * D].rearrange("p (b d) -> p b d", b=TB)
        z_half = work[:, 0:half].rearrange("p (c t) -> p c t", c=EC)
        y_half = work[:, half:2 * half].rearrange("p (q e) -> p q e", q=QB)
        dx_half = work[:, 2 * half:2 * half + 2 * BANK].rearrange("p (k t) -> p k t", k=2)
        h1 = work[:, 0:2 * half].rearrange("p (g m t) -> p g m t", g=2, m=HC)
        mix_t = work[0:NX, 2 * half:2 * half + L]

        decay = sb("decay", [P, N_DECAY, L])
        h_t = [ctx.enter_context(nc.psum_tensor(f"h_t{i}", [P, ED], F32)) for i in range(N_H_T)]
        side = [ctx.enter_context(nc.psum_tensor(f"side{i}", [P, BANK], F32)) for i in range(N_SIDE)]

        b_dram = nc.dram_tensor("b_dram", [2, N, L], F32, kind="Internal").ap()
        xn_dram = nc.dram_tensor("xn_dram", [2, P, DC * L], F32, kind="Internal").ap()
        xz_dram = nc.dram_tensor("xz_dram", [EC, P, L], F32, kind="Internal").ap()
        dx_dram = nc.dram_tensor("dx_dram", [2, EC, P, L], F32, kind="Internal").ap()
        y_dram = nc.dram_tensor("y_dram", [L, ED], F32, kind="Internal").ap()
        x1_dram = nc.dram_tensor("x1_dram", [P, TB * D], F32, kind="Internal").ap()

        pe, dve, act, pool, sp = (Lane(e) for e in (nc.tensor, nc.vector, nc.scalar, nc.gpsimd, nc.sync))

        m_const = mark("m_const", 16)
        m_ident = mark("m_ident")
        m_neg_a = mark("m_neg_a")
        m_setup_pool = mark("m_setup_pool")
        m_decay = mark("m_decay")
        m_drive = mark("m_drive")
        m_scan = mark("m_scan")
        m_turn = mark("m_turn")
        m_y = mark("m_y")
        m_dt_mm = mark("m_dt_mm")
        m_dt_act = mark("m_dt_act")
        m_delta = mark("m_delta")
        m_u = mark("m_u")
        m_brow = [mark(f"m_brow{i}", 16) for i in range(N_B_ROW)]
        m_bdram = mark("m_bdram", 16)
        m_ydump = [mark(f"m_ydump{i}", 16) for i in range(TB)]
        m_side_mm = mark("m_side_mm")
        m_side_act = mark("m_side_act")
        m_side_dve = mark("m_side_dve")
        m_side_pool = mark("m_side_pool")
        m_tok = mark("m_tok", 16)
        m_xnst = mark("m_xnst", 16)
        m_xnld = mark("m_xnld", 16)
        m_dxst = [mark(f"m_dxst{k}", 16) for k in range(2)]
        m_pdxld = [mark(f"m_pdxld{k}", 16) for k in range(2)]
        m_ptok = mark("m_ptok", 16)
        m_dxld = [mark(f"m_dxld{k}", 16) for k in range(2)]
        m_yld = mark("m_yld", 16)
        m_xzst = mark("m_xzst", 16)
        m_xzld = mark("m_xzld", 16)
        m_x1st = mark("m_x1st", 16)
        m_x1ld = mark("m_x1ld", 16)
        m_ew = [mark(f"m_ew{i}", 16) for i in range(3)]
        m_out = mark("m_out", 16)

        loads = [
            (w_in_sb[:, :, :], w_in_t.rearrange("(c p) e -> p c e", p=P)),
            (chan_sb[:, :, :], chan.rearrange("(c p) k -> p c k", p=P)),
            (wx_sb[:, 0, :, :], wx_t[0].rearrange("(c p) k -> p c k", p=P)),
            (wx_sb[:, 1, :, :], wx_t[1].rearrange("(c p) k -> p c k", p=P)),
            (wdt_sb[:, 0, :], wdt_t[0]),
            (wdt_sb[:, 1, :], wdt_t[1]),
            (w_out_sb[:, :, :], w_out_t.rearrange("(c p) d -> p c d", p=P)),
            (router_sb[:, :, :], router_w.rearrange("(c p) e -> p c e", p=P)),
            (router_b_sb[:, :], router_b.rearrange("(a e) -> a e", a=1).to_broadcast([P, E])),
            (b1_sb[:, :, :], b1_t.rearrange("(m p) x -> p m x", p=P)),
            (b2_sb[:, :], b2),
        ]
        for dst, src in loads:
            consts = m_const.on(sp.e.dma_start(dst, src))

        pool.need(m_ident.on(pool.e.memset(ident[:, :], 0.0)))
        ident_ready = m_ident.on(pool.e.affine_select(
            out=ident[:, :], in_=ident[:, :], compare_op=ALU.not_equal, fill=1.0, base=0,
            pattern=[[-1, P]], channel_multiplier=1))
        minus_half_ready = m_setup_pool.on(pool.e.memset(minus_half[:, :], -0.5))
        for e in range(E):
            rank_ready = m_setup_pool.on(pool.e.memset(rank[:, :, e:e + 1], float(E - e)))
        ones_ready = m_setup_pool.on(pool.e.memset(mix[:, :, E:NX], 1.0))

        act.e.preload_act_table_set("natural_log_exp_and_others")
        act.need(consts)
        for d in range(2):
            k = d * NCH + CHAN_A
            ea = m_neg_a.on(act.e.activation(neg_a[:, :, d, :], chan_sb[:, :, k:k + N], ACT.Exp))
        act.need(ea)
        neg_a_ready = m_neg_a.on(act.e.mul(neg_a[:, :, :, :], neg_a[:, :, :, :], -1.0))

        def chan_col(d, c, k):
            return chan_sb[:, c, d * NCH + k:d * NCH + k + 1]

        bank_free = [None] * N_SIDE
        bank_held = [False] * N_SIDE
        bank_next = [0]

        def take_bank():
            i = next(j % N_SIDE for j in range(bank_next[0], bank_next[0] + N_SIDE) if not bank_held[j % N_SIDE])
            bank_next[0] = (i + 1) % N_SIDE
            bank_held[i] = True
            pe.need(bank_free[i])
            return i

        def give_bank(i, token):
            bank_free[i] = token
            bank_held[i] = False

        def products(dst, pairs, m):
            for i, (lhs, rhs) in enumerate(pairs):
                last = pe.e.matmul(dst, lhs, rhs, start=(i == 0), stop=(i == len(pairs) - 1))
            return m.on(last)

        def turns(items, m):
            for dst, src in items:
                k = src.shape[0]
                last = pe.e.transpose(dst, src, ident[0:k, 0:k])
            return m.on(last)

        decay_done, drive_done, scan_done = {}, {}, {}
        turn_done, y_done = {}, {}
        delta_ready, u_ready, x_ready, x_read = {}, {}, {}, {}
        dbc_ready, dbc_read, c_ready, b_stored, b_row_ready = {}, {}, {}, {}, {}
        y_dumped, y_loaded = {}, {}
        xz_stored, xz_loaded = {}, {}
        tick = [0]
        xn_ready, xn_stored, xn_loaded = {}, {}, {}
        dx_stored, dx_loaded = {}, {}
        xn_t_read = [None]
        work_read = []
        prep_read = []
        acc_read = [None]
        xn2_read = [None]
        x1_loaded = [None]
        x1_stored = [None]
        mix_read = [None]

        def hand_over(*marks):
            work_read[:] = [m for m in marks if m is not None]

        def before(done, k):
            return done[k] if k >= 0 else None

        def start_chunk(w, c):
            b, d = divmod(w, 2)
            banks = []
            for s in range(NH):
                i = take_bank()
                pe.need(dbc_ready[w])
                mm = products(side[i][:, :], [(wdt_sb[:, d, c * P:(c + 1) * P],
                                               dbc[0:DTR, s * BANK:(s + 1) * BANK])], m_dt_mm)
                banks.append((i, mm))
            dbc_read[w] = mm
            yield
            for s, (i, mm) in enumerate(banks):
                act.need(mm, decay_done.get(w * UNITS - EC + c))
                pre = m_dt_act.on(act.e.activation(delta[:, c, s * BANK:(s + 1) * BANK], side[i][:, :],
                                                   ACT.Identity, bias=chan_col(d, c, CHAN_B_DT)))
                give_bank(i, pre)
            yield
            log_part = dx_buf[c % 2]
            act.need(pre, delta_ready.get((w, c - 2)), delta_ready.get((w - 1, EC - 1)), *prep_read)
            tmp = m_dt_act.on(act.e.activation(log_part, delta[:, c, :], ACT.Abs))
            act.need(tmp)
            tmp = m_dt_act.on(act.e.activation(log_part, log_part, ACT.Exp, scale=-1.0))
            act.need(tmp)
            tmp = m_dt_act.on(act.e.activation(log_part, log_part, ACT.Ln, bias=1.0))
            yield
            dve.need(tmp)
            delta_ready[w, c] = delta_ready["last"] = m_delta.on(dve.e.scalar_tensor_tensor(
                out=delta[:, c, :], in0=delta[:, c, :], scalar=0.0, in1=log_part, op0=ALU.max, op1=ALU.add))
            pool.need(delta_ready[w, c], x_ready[w], x_read[w])
            u_ready[w, c] = m_u.on(pool.e.tensor_tensor(xu[:, d, c, :], xu[:, d, c, :], delta[:, c, :], ALU.mult))

        def load_b_row(gn):
            w, n = divmod(gn, N)
            sp.need(b_stored[w], before(drive_done, (gn - N_B_ROW) * EC + EC - 1))
            b_row_ready[gn] = m_brow[gn % N_B_ROW].on(sp.e.dma_start(
                b_row[:, gn % N_B_ROW, :], b_dram[w % 2, n:n + 1, :].to_broadcast([P, L])))

        def feed_unit(k):
            gn, c = divmod(k, EC)
            w, n = divmod(gn, N)
            d = w % 2
            act.need(neg_a_ready, delta_ready[w, c], before(scan_done, k - N_DECAY))
            decay_done[k] = m_decay.on(act.e.activation(decay[:, k % N_DECAY, :], delta[:, c, :], ACT.Exp,
                                                        scale=neg_a[:, c, d, n:n + 1]))
            pool.need(u_ready[w, c], b_row_ready[gn], before(scan_done, k - N_DRIVE))
            drive_done[k] = m_drive.on(pool.e.tensor_tensor(drive[:, k % N_DRIVE, :], xu[:, d, c, :],
                                                            b_row[:, gn % N_B_ROW, :], ALU.mult))

        def scan_unit(k):
            gn, c = divmod(k, EC)
            d = (gn // N) % 2
            dve.need(decay_done[k], drive_done[k], before(turn_done, (gn - 2) * TB + TB - 1))
            o, a, v = h[:, gn % 2, c, :], decay[:, k % N_DECAY, :], drive[:, k % N_DRIVE, :]
            if d:
                o, a, v = h[:, gn % 2, c, ::-1], decay[:, k % N_DECAY, ::-1], drive[:, k % N_DRIVE, ::-1]
            scan_done[k] = m_scan.on(dve.e.tensor_tensor_scan(o, a, v, 0.0, ALU.mult, ALU.add))

        def turn_tile(i):
            gn, tb = divmod(i, TB)
            pe.need(ident_ready, scan_done[gn * EC + EC - 1], before(y_done, i - N_H_T))
            turn_done[i] = turns([(h_t[i % N_H_T][:, c * P:(c + 1) * P],
                                   h[:, gn % 2, c, tb * P:(tb + 1) * P]) for c in range(EC)], m_turn)

        def sum_tile(i):
            gn, tb = divmod(i, TB)
            w, n = divmod(gn, N)
            b, d = divmod(w, 2)
            c_n = c_col[:, w % 2, tb, n:n + 1]
            if d == 0 and n == 0:
                dve.need(turn_done[i], c_ready[w], y_dumped.get((b - 1, tb)))
                y_done[i] = m_y.on(dve.e.tensor_scalar(y[:, tb, :], h_t[i % N_H_T][:, :], c_n, None, ALU.mult))
            else:
                dve.need(turn_done[i], c_ready[w], y_done[i - TB])
                y_done[i] = m_y.on(dve.e.scalar_tensor_tensor(
                    out=y[:, tb, :], in0=h_t[i % N_H_T][:, :], scalar=c_n, in1=y[:, tb, :],
                    op0=ALU.mult, op1=ALU.add))
            if d == 1 and n == N - 1:
                sp.need(y_done[i], y_loaded.get((b - 1, tb)))
                y_dumped[b, tb] = m_ydump[tb].on(sp.e.dma_start(y_dram[tb * P:(tb + 1) * P, :], y[:, tb, :]))

        def paced(jobs):
            waiting = []

            def read_first():
                start, read, args, wait = waiting[0]
                while wait and tick[0] < start + READ_LAG:
                    yield None
                waiting.pop(0)
                read(*args)

            for job in jobs:
                if job is None:
                    while waiting:
                        yield from read_first()
                    for _ in range(BARRIER_LAG):
                        yield None
                    continue
                if job == PAUSE:
                    yield None
                    continue
                produce, read, cost = job
                waiting.append((tick[0], read, produce() if produce else (), bool(produce)))
                yield cost
                if len(waiting) > 1:
                    yield from read_first()
            while waiting:
                yield from read_first()
            for _ in range(BARRIER_LAG):
                yield None

        def together(*streams):
            streams = list(streams)
            while streams:
                for stream in list(streams):
                    step = next(stream, "end")
                    if step == "end":
                        streams.remove(stream)
                    else:
                        yield step

        def norm_tokens(src, dst, token, scratch):
            stats, mv, rstd = norm_scratch[scratch]
            n = src.shape[1]
            dve.need(token)
            for tb in range(n):
                st = m_side_dve.on(dve.e.bn_stats(stats[:, tb, :], src[:, tb, :]))
                if tb % 2:
                    yield NORM_COST
            dve.need(st)
            for tb in range(n):
                st = m_side_dve.on(dve.e.bn_aggr(mv[:, tb, :], stats[:, tb, :]))
            dve.need(st)
            st = m_side_dve.on(dve.e.tensor_scalar(rstd[:, 0:n], mv[:, 0:n, 1], EPS, None, ALU.add))
            pool.need(st, minus_half_ready)
            r = m_side_pool.on(pool.e.tensor_tensor(rstd[:, 0:n], rstd[:, 0:n], minus_half[:, 0:n], ALU.pow))
            yield None
            yield None
            dve.need(r)
            for tb in range(n):
                st = m_side_dve.on(dve.e.tensor_scalar(dst[:, tb, :], src[:, tb, :], mv[:, tb, 0:1],
                                                       rstd[:, tb:tb + 1], ALU.subtract, ALU.mult))
                if tb % 2:
                    yield NORM_COST
            return st

        def turn_tokens(src, dst, at, token, dst_free):
            last = {}

            def jobs():
                for c in range(DC):
                    for s in range(src.shape[1] // QB):
                        def produce(c=c, s=s):
                            i = take_bank()
                            pe.need(token, ident_ready)
                            last["turned"] = turns([
                                (side[i][:, q * P:(q + 1) * P], src[:, s * QB + q, c * P:(c + 1) * P])
                                for q in range(QB)], m_side_mm)
                            return i, last["turned"]

                        def read(i, t, c=c, s=s):
                            act.need(t, dst_free)
                            last["copied"] = m_side_act.on(act.e.copy(
                                dst[:, c, at + s * BANK:at + (s + 1) * BANK], side[i][:, :]))
                            give_bank(i, last["copied"])

                        yield produce, read, 0.5

            yield from paced(jobs())
            return last["turned"], last["copied"]

        def prepare(w):
            b, d = divmod(w, 2)
            busy = (*prep_read, delta_ready.get("last"))
            tokens_turned = None
            if d == 0:
                for s in range(NH):
                    sp.need(tokens_turned, *busy)
                    t = m_ptok.on(sp.e.dma_start(prep_tokens[:, :, :], x[b, s * BANK:(s + 1) * BANK, :].rearrange(
                        "(b p) d -> p b d", p=P)))
                    yield None
                    normed = yield from norm_tokens(prep_tokens, prep_tokens, t, 0)
                    tokens_turned, xn_ready[b] = yield from turn_tokens(prep_tokens, xn_t, s * BANK, normed, xn_t_read[0])
                sp.need(xn_ready[b], xn_loaded.get(b - 2))
                xn_stored[b] = m_xnst.on(sp.e.dma_start(xn_dram[b % 2], xn_t[:, :, :].rearrange("p c t -> p (c t)")))
            pool.need(*busy)
            pool.e.memset(xz_pad[:, 0:PAD], 0.0)
            pads = m_side_pool.on(pool.e.memset(xz_pad[:, PAD + L:XZW], 0.0))
            buffer_free = drive_done.get((w - 1) * UNITS - 1)
            starts = [PAD + (TAPS - 1 - k) * (1 if d else -1) for k in range(TAPS)]
            got = {}
            pe.need(consts)

            def load_xz(c):
                sp.need(xz_stored[b, c], got.get("tap"), pads, *busy)
                got[c] = xz_loaded[b, c] = m_xzld.on(sp.e.dma_start(xz_pad[:, PAD:PAD + L], xz_dram[c]))

            def project_jobs():
                for c in range(EC):
                    if d == 1:
                        yield None, (lambda c=c: load_xz(c)), 0.1
                        yield None
                    else:
                        for s in range(NH):
                            def produce(c=c, s=s):
                                i = take_bank()
                                pe.need(xn_ready[b])
                                xn_t_read[0] = products(side[i][:, :], [
                                    (w_in_sb[:, k, c * P:(c + 1) * P], xn_t[:, k, s * BANK:(s + 1) * BANK])
                                    for k in range(DC)], m_side_mm)
                                return i, xn_t_read[0]

                            def read(i, mm, c=c, s=s):
                                act.need(mm, got.get("tap"), xz_stored.get((b, c - 1)), *busy)
                                got[c] = m_side_act.on(act.e.copy(
                                    xz_pad[:, PAD + s * BANK:PAD + (s + 1) * BANK], side[i][:, :]))
                                give_bank(i, got[c])
                                if s == NH - 1:
                                    sp.need(got[c], xz_loaded.get((b - 1, c)))
                                    xz_stored[b, c] = m_xzst.on(sp.e.dma_start(xz_dram[c], xz_pad[:, PAD:PAD + L]))

                            yield produce, read, 1.8
                    for k in range(TAPS):
                        def tap(c=c, k=k):
                            zb = xz_pad[:, starts[k]:starts[k] + L]
                            if k == 0:
                                act.need(got[c], pads, buffer_free)
                                got["first tap"] = m_side_act.on(act.e.activation(
                                    xu[:, d, c, :], zb, ACT.Identity, scale=chan_col(d, c, CHAN_CONV_W),
                                    bias=chan_col(d, c, CHAN_CONV_B)))
                            else:
                                dve.need(got["first tap"], got.get("tap"))
                                got["tap"] = m_side_dve.on(dve.e.scalar_tensor_tensor(
                                    out=xu[:, d, c, :], in0=zb, scalar=chan_col(d, c, CHAN_CONV_W + k),
                                    in1=xu[:, d, c, :], op0=ALU.mult, op1=ALU.add))

                        yield None, tap, TAP_COST

            yield from paced(project_jobs())
            if d == 0 and b:
                load_xn(b - 1)
            act.need(got["tap"])
            x_ready[w] = m_side_act.on(act.e.activation(xu[:, d, :, :], xu[:, d, :, :], ACT.Silu))
            act.e.preload_act_table_set("natural_log_exp_and_others")
            yield None
            yield None
            yield None

            def later_jobs():
                for s in range(NH):
                    def produce(s=s):
                        i = take_bank()
                        pe.need(x_ready[w])
                        x_read[w] = products(side[i][0:NP, :], [
                            (wx_sb[:, d, c, :], xu[:, d, c, s * BANK:(s + 1) * BANK]) for c in range(EC)], m_side_mm)
                        return i, x_read[w]

                    def read(i, mm, s=s):
                        act.need(mm, dbc_read.get(w - 1), b_stored.get(w - 1), c_ready.get(w - 1))
                        dbc_ready[w] = m_side_act.on(act.e.copy(dbc[:, s * BANK:(s + 1) * BANK], side[i][0:NP, :]))
                        give_bank(i, dbc_ready[w])

                    yield produce, read, 3.6
                for c in range(EC):
                    def load_dx(c=c):
                        sp.need(x_ready[w], dx_stored[w - 1, c], dx_stored.get((w, c - 2)))
                        got["dx", c] = m_pdxld[c % 2].on(sp.e.dma_start(dx_buf[c % 2], dx_dram[b % 2, c]))

                    def scale_by_d(c=c):
                        buf = dx_buf[c % 2]
                        if d == 0:
                            act.need(x_ready[w], tokens_turned, xz_stored[b, EC - 1], dx_stored.get((w, c - 2)), *busy)
                            r = m_side_act.on(act.e.mul(buf, xu[:, d, c, :], chan_col(d, c, CHAN_D)))
                        else:
                            dve.need(x_ready[w], got["dx", c])
                            r = m_side_dve.on(dve.e.scalar_tensor_tensor(
                                out=buf, in0=xu[:, d, c, :], scalar=chan_col(d, c, CHAN_D), in1=buf,
                                op0=ALU.mult, op1=ALU.add))
                        sp.need(r, *(dx_loaded.get((b - 2, k)) for k in range(2)))
                        dx_stored[w, c] = m_dxst[c % 2].on(sp.e.dma_start(dx_dram[b % 2, c], buf))

                    if d == 1:
                        if c == 0:
                            load_dx(0)
                        if c + 1 < EC:
                            yield None, (lambda c=c: load_dx(c + 1)), 0.1
                        yield None
                    yield None, scale_by_d, 0.5
                yield None
                sp.need(dbc_ready[w], *(b_row_ready.get((w - 1) * N - 1 - i) for i in range(N_B_ROW)))
                b_stored[w] = m_bdram.on(sp.e.dma_start(b_dram[w % 2], dbc[DTR:DTR + N, :]))
                for s in range(NH):
                    def produce(s=s):
                        i = take_bank()
                        pe.need(dbc_ready[w])
                        return i, turns([(side[i][:, q * NP:(q + 1) * NP],
                                          dbc[:, (s * QB + q) * P:(s * QB + q + 1) * P]) for q in range(QB)], m_side_mm)

                    def read(i, t, s=s):
                        act.need(t, y_done.get((w - 1) * N * TB - 1))
                        c_ready[w] = m_side_act.on(act.e.copy(
                            c_col[:, w % 2, s * QB:(s + 1) * QB, :],
                            side[i][:, 0:QB * NP].rearrange("p (q k) -> p q k", q=QB)[:, :, DTR + N:NP]))
                        give_bank(i, c_ready[w])

                    yield produce, read, 0.5

            yield from paced(later_jobs())
            prep_read[:] = [got["tap"], dx_stored[w, EC - 2], dx_stored[w, EC - 1], xz_stored[b, EC - 1]]

        def load_xn(b):
            sp.need(xn_t_read[0], xn_stored[b], xn_stored.get(b + 1))
            xn_loaded[b] = m_xnld.on(sp.e.dma_start(xn_t[:, :, :].rearrange("p c t -> p (c t)"), xn_dram[b % 2]))

        def gate(b):
            busy = tuple(work_read)
            if b not in xn_loaded:
                load_xn(b)
            got = {}

            def load_y(s):
                rows = y_dram[s * BANK:(s + 1) * BANK, :].rearrange("(q p) e -> p q e", p=P)
                sp.need(*(y_dumped[b, s * QB + q] for q in range(QB)), got.get("y turned"), *busy)
                got["y", s] = m_yld.on(sp.e.dma_start(y_half[:, :, :], rows))
                for q in range(QB):
                    y_loaded[b, s * QB + q] = got["y", s]

            def load_dx(j):
                s, c = divmod(j, EC)
                sp.need(dx_stored[2 * b + 1, c], got.get("gated"), *busy)
                got["dx", j] = dx_loaded[b, j % 2] = m_dxld[j % 2].on(sp.e.dma_start(
                    dx_half[:, j % 2, :], dx_dram[b % 2, c, :, s * BANK:(s + 1) * BANK]))

            def jobs():
                load_y(0)
                load_dx(0)
                load_dx(1)
                for s in range(NH):
                    for c in range(EC):
                        def produce(s=s, c=c):
                            i = take_bank()
                            pe.need(xn_loaded[b])
                            got["z mm"] = products(side[i][:, :], [
                                (w_in_sb[:, k, ED + c * P:ED + (c + 1) * P], xn_t[:, k, s * BANK:(s + 1) * BANK])
                                for k in range(DC)], m_side_mm)
                            return i, got["z mm"]

                        def read(i, mm, c=c):
                            act.need(mm, got.get("projected"), *busy)
                            got["z"] = m_side_act.on(act.e.copy(z_half[:, c, :], side[i][:, :]))
                            give_bank(i, got["z"])
                            if c == EC - 1:
                                act.need(got["z"])
                                got["z"] = m_side_act.on(act.e.activation(z_half[:, :, :], z_half[:, :, :], ACT.Silu))
                                act.e.preload_act_table_set("natural_log_exp_and_others")

                        yield produce, read, 1.8
                    for c in range(EC):
                        def produce(s=s, c=c):
                            i = take_bank()
                            pe.need(got["y", s])
                            got["y turned"] = turns([(side[i][:, q * P:(q + 1) * P], y_half[:, q, c * P:(c + 1) * P])
                                                     for q in range(QB)], m_side_mm)
                            return i, got["y turned"]

                        def add(i, t, s=s, c=c):
                            j = s * EC + c
                            a = dx_half[:, j % 2, :]
                            dve.need(t, got["dx", j])
                            v = m_side_dve.on(dve.e.tensor_tensor(a, side[i][:, :], a, ALU.add))
                            give_bank(i, v)
                            pool.need(v, got["z"])
                            got["gated"] = m_side_pool.on(pool.e.tensor_tensor(
                                z_half[:, c, :], z_half[:, c, :], a, ALU.mult))
                            if j + 2 < NH * EC:
                                load_dx(j + 2)

                        yield produce, add, 0.8
                    yield None
                    if s + 1 < NH:
                        load_y(s + 1)
                    for q in range(QB):
                        def produce(q=q):
                            i = take_bank()
                            pe.need(got["gated"])
                            got["projected"] = products(side[i][:, 0:D], [
                                (z_half[:, c, q * P:(q + 1) * P], w_out_sb[:, c, :]) for c in range(EC)], m_side_mm)
                            return i, got["projected"]

                        def read(i, mm, tb=s * QB + q):
                            act.need(mm, acc_read[0])
                            got["o"] = m_side_act.on(act.e.mul(acc[:, tb, :], side[i][:, 0:D], 0.5))
                            give_bank(i, got["o"])

                        yield produce, read, 1.8

            yield from paced(jobs())
            xn_t_read[0] = got["z mm"]
            if b == NB - 2:
                load_xn(NB - 1)
            sp.need(got["projected"])
            t = m_tok.on(sp.e.dma_start(tokens[:, :, :], x[b].rearrange("(b p) d -> p b d", p=P)))
            normed = yield from norm_tokens(acc, acc, got["o"], 1)
            dve.need(normed, t)
            for q in range(0, TB, 2):
                r = m_side_dve.on(dve.e.tensor_tensor(acc[:, q:q + 2, :], acc[:, q:q + 2, :], tokens[:, q:q + 2, :],
                                                      ALU.add))
                yield NORM_COST
            sp.need(r, x1_loaded[0])
            x1_stored[0] = m_x1st.on(sp.e.dma_start(x1_dram, acc[:, :, :].rearrange("p b d -> p (b d)")))
            yield None
            normed = yield from norm_tokens(acc, tokens, r, 1)
            tokens_turned, xn2_ready[0] = yield from turn_tokens(tokens, xn2_t, 0, normed, xn2_read[0])
            hand_over(tokens_turned)

        xn2_ready = [None]

        def route(b):
            busy = tuple(work_read)
            i = take_bank()
            pe.need(xn2_ready[0])
            for tb in range(TB):
                lg = products(side[i][:, tb * E:(tb + 1) * E],
                              [(xn2_t[:, k, tb * P:(tb + 1) * P], router_sb[:, k, :]) for k in range(DC)], m_side_mm)
            yield 1.5
            dve.need(lg)
            v = m_side_dve.on(dve.e.tensor_tensor(
                logits[:, :, :], side[i][:, 0:TB * E].rearrange("p (b e) -> p b e", b=TB),
                router_b_sb[:, :].rearrange("p (a e) -> p a e", a=1).to_broadcast([P, TB, E]), ALU.add))
            give_bank(i, v)

            def step(instruction):
                v = m_side_dve.on(instruction)
                dve.need(v)
                return v

            def wide():
                return peak[:, :].rearrange("p (b a) -> p b a", a=1).to_broadcast([P, TB, E])

            dve.need(v)
            step(dve.e.tensor_reduce(peak[:, :], logits[:, :, :], AX_X, ALU.max))
            v = step(dve.e.tensor_tensor(logits[:, :, :], logits[:, :, :], wide(), ALU.subtract))
            act.need(v)
            v = m_side_act.on(act.e.activation(logits[:, :, :], logits[:, :, :], ACT.Exp))
            yield None
            yield None
            dve.need(v)
            step(dve.e.tensor_reduce(peak[:, :], logits[:, :, :], AX_X, ALU.add))
            step(dve.e.reciprocal(peak[:, :], peak[:, :]))
            step(dve.e.tensor_tensor(logits[:, :, :], logits[:, :, :], wide(), ALU.mult))
            dve.need(rank_ready, ones_ready, mix_read[0])

            def first_of_largest(p, sel):
                step(dve.e.tensor_reduce(peak[:, :], p, AX_X, ALU.max))
                step(dve.e.tensor_tensor(cand[:, :, :], p, wide(), ALU.is_equal))
                step(dve.e.tensor_tensor(cand[:, :, :], cand[:, :, :], rank[:, :, :], ALU.mult))
                step(dve.e.tensor_reduce(peak[:, :], cand[:, :, :], AX_X, ALU.max))
                step(dve.e.tensor_tensor(sel, cand[:, :, :], wide(), ALU.is_equal))

            first_of_largest(logits[:, :, :], sel1[:, :, :])
            yield None
            step(dve.e.scalar_tensor_tensor(out=mix[:, :, 0:E], in0=sel1[:, :, :], scalar=-2.0,
                                            in1=logits[:, :, :], op0=ALU.mult, op1=ALU.add))
            first_of_largest(mix[:, :, 0:E], sel2[:, :, :])
            step(dve.e.tensor_tensor(sel1[:, :, :], sel1[:, :, :], sel2[:, :, :], ALU.add))
            mixed = step(dve.e.tensor_tensor(mix[:, :, 0:E], logits[:, :, :], sel1[:, :, :], ALU.mult))
            yield None
            mix_ready[b] = mixed
            for q in range(0, TB, QB):
                i = take_bank()
                pe.need(mixed)
                t = turns([(side[i][0:NX, r * P:(r + 1) * P], mix[:, q + r, :]) for r in range(QB)], m_side_mm)
                yield 0.5
                yield None
                act.need(t, *busy)
                mix_t_ready[b] = m_side_act.on(act.e.copy(mix_t[:, q * P:q * P + BANK], side[i][0:NX, :]))
                give_bank(i, mix_t_ready[b])

        mix_ready, mix_t_ready = {}, {}
        acc_done = {}
        expert_loaded, expert_read = {}, {}

        def load_expert(s):
            if s >= 2 * NX * NB or s in expert_loaded:
                return
            xp, k = divmod(s % (2 * NX), 2)
            src = w1[xp].rearrange("(c p) n -> p c n", p=P) if k == 0 else w2[xp].rearrange("(c p) n -> p c n", p=P)
            sp.need(expert_read.get(s - 3))
            expert_loaded[s] = m_ew[s % 3].on(sp.e.dma_start(
                expert_w[:, s % 3, :].rearrange("p (c n) -> p c n", n=src.shape[2]), src))

        h1_read = [None, None]

        def experts(b):
            busy = tuple(work_read)
            hid = {}
            last_read = {}

            def jobs():
                for xp in range(NX):
                    s = 2 * (b * NX + xp)
                    load_expert(s)
                    load_expert(s + 1)
                    wi = expert_w[:, s % 3, :].rearrange("p (c n) -> p c n", n=H)
                    wo = expert_w[:, (s + 1) % 3, :].rearrange("p (c n) -> p c n", n=D)
                    for g in range(NH):
                        for m in range(HC):
                            def produce(s=s, wi=wi, g=g, m=m):
                                i = take_bank()
                                pe.need(expert_loaded[s], xn2_ready[0])
                                mm = products(side[i][:, :], [(wi[:, k, m * P:(m + 1) * P],
                                                               xn2_t[:, k, g * BANK:(g + 1) * BANK])
                                                              for k in range(DC)], m_side_mm)
                                if g == NH - 1 and m == HC - 1:
                                    expert_read[s] = mm
                                    load_expert(s + 2)
                                return i, mm

                            def read(i, mm, xp=xp, g=g, m=m):
                                act.need(mm, h1_read[g], *busy)
                                e = m_side_act.on(act.e.activation(h1[:, g, m, :], side[i][:, :], ACT.Identity,
                                                                   bias=b1_sb[:, m, xp:xp + 1]))
                                give_bank(i, e)
                                if m == HC - 1:
                                    act.need(e)
                                    hid[g] = m_side_act.on(act.e.activation(h1[:, g, :, :], h1[:, g, :, :], ACT.Gelu))
                                    act.e.preload_act_table_set("natural_log_exp_and_others")

                            yield produce, read, 1.8
                    while b not in mix_ready:
                        yield PAUSE
                    for g in range(NH):
                        for q in range(QB):
                            def produce(s=s, wo=wo, g=g, q=q, xp=xp):
                                i = take_bank()
                                pe.need(hid[g], expert_loaded[s + 1])
                                pairs = [(h1[:, g, m, q * P:(q + 1) * P], wo[:, m, :]) for m in range(HC)]
                                if xp == NX - 1:
                                    pe.need(mix_t_ready[b])
                                    tb = g * QB + q
                                    pairs.append((mix_t[:, tb * P:(tb + 1) * P], b2_sb[:, :]))
                                mm = products(side[i][:, 0:D], pairs, m_side_mm)
                                if q == QB - 1:
                                    h1_read[g] = expert_read[s + 1] = mm
                                last_read[0] = mm
                                return i, mm

                            def read(i, mm, xp=xp, tb=g * QB + q):
                                if xp == 0:
                                    dve.need(mm, mix_ready[b], x1_stored[0])
                                    op = dve.e.tensor_scalar(acc[:, tb, :], side[i][:, 0:D], mix[:, tb, 0:1], None,
                                                             ALU.mult)
                                else:
                                    dve.need(mm, acc_done[tb])
                                    op = dve.e.scalar_tensor_tensor(
                                        out=acc[:, tb, :], in0=side[i][:, 0:D], scalar=mix[:, tb, xp:xp + 1],
                                        in1=acc[:, tb, :], op0=ALU.mult, op1=ALU.add)
                                acc_done[tb] = m_side_dve.on(op)
                                give_bank(i, acc_done[tb])

                            yield produce, read, 1.8

            yield from paced(jobs())
            hand_over(*busy, last_read[0])
            xn2_read[0] = last_read[0]
            mix_read[0] = acc_done[TB - 1]

        def finish(b):
            busy = tuple(work_read)
            sp.need(x1_stored[0], *busy)
            x1_loaded[0] = m_x1ld.on(sp.e.dma_start(tokens[:, :, :].rearrange("p b d -> p (b d)"), x1_dram))
            normed = yield from norm_tokens(acc, acc, acc_done[TB - 1], 1)
            dve.need(normed, x1_loaded[0])
            for q in range(0, TB, 2):
                r = m_side_dve.on(dve.e.tensor_tensor(acc[:, q:q + 2, :], acc[:, q:q + 2, :], tokens[:, q:q + 2, :],
                                                      ALU.add))
                yield NORM_COST
            sp.need(r)
            acc_read[0] = m_out.on(sp.e.dma_start(out[b].rearrange("(b p) d -> p b d", p=P), acc[:, :, :]))
            hand_over(r)

        def expert_stream(b):
            yield from gate(b)
            yield from together(route(b), experts(b))
            yield from finish(b)

        class SideWork:

            def __init__(self, steps, cost, end):
                self.steps, self.left, self.end, self.credit = steps, cost, end, 0.0

            def advance(self, now):
                self.credit = min(self.credit + max(self.left, 0.0) / max(self.end - now, 1), MAX_CREDIT)
                while self.credit > 0:
                    step = next(self.steps, "end")
                    if step == "end":
                        self.credit = 0.0
                    elif step is None:
                        break
                    else:
                        self.credit -= step + STEP_COST
                        self.left -= step + STEP_COST

            def finish(self):
                for _ in self.steps:
                    tick[0] += 1

        def start_stages(k):
            for stage, lead in ((3, 1), (2, EC - 2), (1, EC - 1), (0, EC)):
                w, c = divmod(k + lead, UNITS)
                if c < EC and 0 <= w < NW:
                    if stage == 0:
                        starting[w, c] = start_chunk(w, c)
                    next(starting[w, c], None)

        starting = {}

        def feed(k):
            start_stages(k)
            if k % EC == 0 and k + (N_B_ROW - 1) * EC < NU:
                load_b_row(k // EC + N_B_ROW - 1)
            if k < NU:
                feed_unit(k)

        NU = NW * UNITS
        SideWork(prepare(0), 0.0, 0).finish()
        for k in range(-EC, 0):
            start_stages(k)
        for gn in range(N_B_ROW - 1):
            load_b_row(gn)
        for k in range(LOOKAHEAD):
            feed(k)
        tiles_turned = 0
        for k in range(NU + EC):
            w, unit = divmod(k, UNITS)
            if w < NW:
                start = PREP_START[w % 2]
                if unit == start:
                    preparing = SideWork(prepare(w + 1) if w + 1 < NW else iter(()), PREP_COST[w % 2],
                                         2 * ((w + 1) * UNITS - N_B_ROW * EC) - PREP_MARGIN)
                if unit == EC and w % 2 == 0:
                    if w:
                        mixing.finish()
                    mixing = SideWork(expert_stream(w // 2 - 1) if w else iter(()), MIX_COST,
                                      2 * (k + 2 * UNITS) - MIX_MARGIN)
                scan_unit(k)
                feed(k + LOOKAHEAD)
            turnable = min(k // EC if (k + 1) % EC else k // EC + 1, NU // EC) * TB
            for half in range(2):
                i = 2 * (k - EC) + half
                while tiles_turned < min(turnable, i + N_H_T):
                    turn_tile(tiles_turned)
                    tiles_turned += 1
                if i >= 0:
                    sum_tile(i)
                tick[0] += 1
                if w < NW and unit >= start:
                    preparing.advance(2 * k + half)
                if EC <= k < NU:
                    mixing.advance(2 * k + half)
            if w < NW and unit == UNITS - N_B_ROW * EC:
                preparing.finish()
        mixing.finish()
        SideWork(expert_stream(NB - 1), 0.0, 0).finish()
        sp.need((m_out, m_out.count), (m_bdram, m_bdram.count), (m_xnst, m_xnst.count), (m_x1st, m_x1st.count),
                *[(m, m.count) for m in m_dxst], (m_xzst, m_xzst.count), *[(m, m.count) for m in m_ydump])


def kernel(**inputs):
    import numpy as np
    import concourse.bacc as bacc
    from concourse.bass_utils import run_bass_kernel_spmd as run

    a = {k: np.asarray(v) for k, v in inputs.items()}

    def chan(s):
        cols = [a["L0_attn_conv_w" + s][:, 0, :], a["L0_attn_conv_b" + s][:, None], a["L0_attn_b_dt" + s][:, None],
                a["L0_attn_Dp" + s][:, None], a["L0_attn_A_log" + s]]
        return np.concatenate(cols, axis=1)

    arrays = {
        "x": a["L0_attn_x"],
        "w_in_t": a["L0_attn_W_in"].T,
        "chan": np.concatenate([chan(""), chan("_b")], axis=1),
        "wx_t": np.stack([a["L0_attn_Wx"].T, a["L0_attn_Wx_b"].T]),
        "wdt_t": np.stack([a["L0_attn_Wdt"].T, a["L0_attn_Wdt_b"].T]),
        "w_out_t": a["L0_attn_W_out"].T,
        "router_w": a["L0_ffn_router_w"],
        "router_b": a["L0_ffn_router_b"],
        "w1": np.concatenate([a["L0_ffn_rw1"], a["L0_ffn_sw1"][None]]),
        "b1_t": np.concatenate([a["L0_ffn_rb1"], a["L0_ffn_sb1"][None]]).T,
        "w2": np.concatenate([a["L0_ffn_rw2"], a["L0_ffn_sw2"][None]]),
        "b2": np.concatenate([a["L0_ffn_rb2"], a["L0_ffn_sb2"][None]]),
    }
    arrays = {f"in_{k}": np.ascontiguousarray(v) for k, v in arrays.items()}
    nc = bacc.Bacc("TRN2", target_bir_lowering=False, num_devices=1,
                    dynamic_dma_scratch_size=DMA_RING_BYTES)
    args = [nc.dram_tensor(k, v.shape, mybir.dt.from_np(v.dtype), kind="ExternalInput").ap() for k, v in arrays.items()]
    out = nc.dram_tensor("out", a["L0_attn_x"].shape, F32, kind="ExternalOutput").ap()
    mamba_moe(nc, *args, out)
    r = run(nc, [arrays], core_ids=[0])
    return r.results[0]["out"]
```
